# Optimizing a Trainium2 kernel written in Bass

```python
import numpy as np
import jax
import jax.numpy as jnp

def _softmax(x, axis=-1):
    return jax.nn.softmax(x, axis=axis)

def _gelu(x):
    return jax.nn.gelu(x, approximate=True)

def _silu(x):
    return jax.nn.silu(x)

def _sigmoid(x):
    return jax.nn.sigmoid(x)

def _layernorm(x, axis=-1, eps=1e-05):
    m = jnp.mean(x, axis=axis, keepdims=True)
    v = jnp.var(x, axis=axis, keepdims=True)
    return (x - m) / jnp.sqrt(v + eps)

def _scatter_add(tgt, idx, src, axis=0):
    return tgt.at[idx].add(src)

def _segment_sum(src, seg, n):
    return jax.ops.segment_sum(src, seg, n)
kernel_name = 'mk_xattn_ffn_d1_seqx_r4_4ddfbb'

def setup_inputs(seed: int=0):
    np.random.seed(seed)
    _w = jnp.asarray

    def _rec_inputs():
        import jax
        import jax.numpy as jnp
        _rk = jax.random.key(seed)
        x = -0.0003929 + 0.9999 * jax.random.normal(jax.random.fold_in(_rk, 1), (4, 512, 512), jnp.float32)
        _lenS = 512 - jax.random.randint(jax.random.fold_in(_rk, 7), (4,), 0, max(1, 512 // 4) + 1, jnp.int32)
        _lenS2 = 64 - jax.random.randint(jax.random.fold_in(_rk, 8), (4,), 0, max(1, 64 // 4) + 1, jnp.int32)
        _ctx_2048P = jax.random.normal(jax.random.fold_in(_rk, 11), (4, 16, 512), jnp.float32)
        _ctx_2048c = jax.random.dirichlet(jax.random.fold_in(_rk, 511), 0.3 * jnp.ones((16,), jnp.float32), (4, 64))
        _ctx_2048t = jnp.einsum('bsk,bkd->bsd', _ctx_2048c, _ctx_2048P)
        _ctx_2048t = _ctx_2048t * jax.lax.rsqrt(jnp.mean(jnp.square(_ctx_2048t)) + 1e-12) * 0.953939
        ctx_2048 = -0.000514642 + 1.00011 * (_ctx_2048t + 0.3 * jax.random.normal(jax.random.fold_in(_rk, 611), (4, 64, 512), jnp.float32))
        _validS = jnp.arange(512)[None, :] < _lenS[:, None]
        _validS2 = jnp.arange(64)[None, :] < _lenS2[:, None]
        _causal = jnp.tril(jnp.ones((512, 512), dtype=bool))
        mask_BxS2_ik0 = jnp.where(jnp.broadcast_to(_validS2[:, :], (4, 64)), 0, 1).astype(jnp.int32)
        return (x, ctx_2048, mask_BxS2_ik0)
    x, ctx_2048, mask_BxS2_ik0 = _rec_inputs()

    def _L0_xattn_setup():
        import jax, jax.numpy as jnp
        import numpy as np
        import math
        H = 512
        NH = 16
        HD = H // NH
        EPS_LN = 1e-05
        RES_SCALE_MAX = 0.3

        def _nan_clean(x, lim=10000.0):
            return jnp.nan_to_num(x, nan=0.0, posinf=lim, neginf=-lim)
        key = jax.random.key(seed)
        ks = jax.random.split(key, 12)
        B, S, T = (4, 512, 64)
        std = 1.0 / math.sqrt(H)
        return {'hidden_states': jax.random.normal(ks[0], (B, S, H), jnp.float32), 'audio_tokens': jax.random.normal(ks[1], (B, T, H), jnp.float32), 'attention_mask': jax.random.randint(ks[2], (B, T), 0, 2, jnp.int32), 'Wq': jax.random.normal(ks[3], (H, H), jnp.float32) * std, 'bq': jnp.zeros((H,), jnp.float32), 'Wk': jax.random.normal(ks[4], (H, H), jnp.float32) * std, 'bk': jnp.zeros((H,), jnp.float32), 'Wv': jax.random.normal(ks[5], (H, H), jnp.float32) * std, 'bv': jnp.zeros((H,), jnp.float32), 'Wo': jax.random.normal(ks[6], (H, H), jnp.float32) * std, 'bo': jnp.zeros((H,), jnp.float32), 'ln_gamma': jnp.ones((H,), jnp.float32), 'ln_beta': jnp.zeros((H,), jnp.float32), 'residual_scale': jnp.float32(0.05)}
    _L0_xattn_all = _L0_xattn_setup()
    _L0_xattn_in = {k: v for k, v in _L0_xattn_all.items() if k in ('Wq', 'bq', 'Wk', 'bk', 'Wv', 'bv', 'Wo', 'bo', 'ln_gamma', 'ln_beta', 'residual_scale')}
    del _L0_xattn_all

    def _L0_ffn_setup():
        import jax, jax.numpy as jnp
        import numpy as np
        H = 512
        E = 8
        K = 2
        I = 16
        key = jax.random.key(seed)
        k1, k2, k3, k4 = jax.random.split(key, 4)
        B, T = (2, 1024)
        x = jax.random.normal(k1, (B, T, H), dtype=jnp.float32)
        router_w = jax.random.normal(k2, (E, H), dtype=jnp.float32) / np.sqrt(H)
        down_w = jax.random.normal(k3, (E, I, H), dtype=jnp.float32) / np.sqrt(H)
        up_w = jax.random.normal(k4, (E, H, I), dtype=jnp.float32) / np.sqrt(I)
        return {'x': x, 'router_w': router_w, 'down_w': down_w, 'up_w': up_w}
    _L0_ffn_all = _L0_ffn_setup()
    _L0_ffn_in = {k: v for k, v in _L0_ffn_all.items() if k in ('router_w', 'down_w', 'up_w')}
    del _L0_ffn_all
    return {'x': x, 'ctx_2048': ctx_2048, 'mask_BxS2_ik0': mask_BxS2_ik0, 'L0_xattn_Wq': _L0_xattn_in['Wq'], 'L0_xattn_bq': _L0_xattn_in['bq'], 'L0_xattn_Wk': _L0_xattn_in['Wk'], 'L0_xattn_bk': _L0_xattn_in['bk'], 'L0_xattn_Wv': _L0_xattn_in['Wv'], 'L0_xattn_bv': _L0_xattn_in['bv'], 'L0_xattn_Wo': _L0_xattn_in['Wo'], 'L0_xattn_bo': _L0_xattn_in['bo'], 'L0_xattn_ln_gamma': _L0_xattn_in['ln_gamma'], 'L0_xattn_ln_beta': _L0_xattn_in['ln_beta'], 'L0_xattn_residual_scale': _L0_xattn_in['residual_scale'], 'L0_ffn_router_w': _L0_ffn_in['router_w'], 'L0_ffn_down_w': _L0_ffn_in['down_w'], 'L0_ffn_up_w': _L0_ffn_in['up_w']}

def reference(x, ctx_2048, mask_BxS2_ik0, L0_xattn_Wq, L0_xattn_bq, L0_xattn_Wk, L0_xattn_bk, L0_xattn_Wv, L0_xattn_bv, L0_xattn_Wo, L0_xattn_bo, L0_xattn_ln_gamma, L0_xattn_ln_beta, L0_xattn_residual_scale, L0_ffn_router_w, L0_ffn_down_w, L0_ffn_up_w):
    import jax
    import jax.numpy as jnp

    def _L0_xattn_ref(hidden_states, audio_tokens, attention_mask, Wq, bq, Wk, bk, Wv, bv, Wo, bo, ln_gamma, ln_beta, residual_scale):
        import jax, jax.numpy as jnp
        import numpy as np
        import math
        H = 512
        NH = 16
        HD = H // NH
        EPS_LN = 1e-05
        RES_SCALE_MAX = 0.3

        def _nan_clean(x, lim=10000.0):
            return jnp.nan_to_num(x, nan=0.0, posinf=lim, neginf=-lim)
        B, S, _ = hidden_states.shape
        T = audio_tokens.shape[1]
        hs = _nan_clean(hidden_states).astype(jnp.float32)
        at = _nan_clean(audio_tokens).astype(jnp.float32)

        def proj(x, W, b, L):
            y = x @ W.T + b
            return y.reshape(B, L, NH, HD).transpose(0, 2, 1, 3)
        q = _nan_clean(proj(hs, Wq, bq, S))
        k = _nan_clean(proj(at, Wk, bk, T))
        v = _nan_clean(proj(at, Wv, bv, T))
        scale = max(math.sqrt(HD), 1e-08)
        scores = jnp.einsum('bhsd,bhtd->bhst', q, k) / scale
        scores = jnp.clip(scores, -50.0, 50.0)
        scores = jnp.nan_to_num(scores, nan=0.0, posinf=50.0, neginf=-50.0)
        attend = (attention_mask.astype(jnp.float32) > 0.5)[:, None, None, :]
        scores = jnp.where(attend, scores, -10000.0)
        scores = jnp.clip(scores, -50.0, 50.0)
        probs = jax.nn.softmax(scores, axis=-1)
        probs = jnp.nan_to_num(probs, nan=0.0, posinf=1.0, neginf=0.0)
        probs = probs / (probs.sum(axis=-1, keepdims=True) + 1e-08)
        ctx = jnp.einsum('bhst,bhtd->bhsd', probs, v)
        ctx = ctx.transpose(0, 2, 1, 3).reshape(B, S, H)
        delta = _nan_clean(ctx @ Wo.T + bo)
        rs = jnp.clip(residual_scale, 0.0, RES_SCALE_MAX)
        delta = rs * delta
        mu = delta.mean(axis=-1, keepdims=True)
        var = jnp.mean((delta - mu) ** 2, axis=-1, keepdims=True)
        delta = (delta - mu) / jnp.sqrt(var + EPS_LN) * ln_gamma + ln_beta
        return delta

    def _L0_ffn_ref(x, router_w, down_w, up_w):
        import jax, jax.numpy as jnp
        import numpy as np
        H = 512
        E = 8
        K = 2
        I = 16
        logits = jnp.einsum('bth,eh->bte', x, router_w)
        weights = jax.nn.softmax(logits, axis=-1)
        top_w, top_idx = jax.lax.top_k(weights, K)
        topk_mask = jnp.sum(jax.nn.one_hot(top_idx, E, dtype=x.dtype), axis=-2)
        gate = weights * topk_mask
        h = jnp.einsum('bth,eih->beti', x, down_w)
        a = jax.nn.silu(h)
        expert_out = jnp.einsum('beti,ehi->beth', a, up_w)
        out = jnp.einsum('beth,bte->bth', expert_out, gate)
        return out
    x = x + _L0_xattn_ref(_layernorm(x, axis=-1), ctx_2048, mask_BxS2_ik0, L0_xattn_Wq, L0_xattn_bq, L0_xattn_Wk, L0_xattn_bk, L0_xattn_Wv, L0_xattn_bv, L0_xattn_Wo, L0_xattn_bo, L0_xattn_ln_gamma, L0_xattn_ln_beta, L0_xattn_residual_scale)
    x = x + _L0_ffn_ref(_layernorm(x, axis=-1), L0_ffn_router_w, L0_ffn_down_w, L0_ffn_up_w)
    return x

_drawn_inputs = setup_inputs


def setup_inputs(seed=0):
    import zlib

    import numpy as np

    out = dict(_drawn_inputs(seed))
    spreads = {'L0_xattn_bq': (0.0, 0.1),
     'L0_xattn_bk': (0.0, 0.1),
     'L0_xattn_bv': (0.0, 0.1),
     'L0_xattn_bo': (0.0, 0.1),
     'L0_xattn_ln_gamma': (1.0, 0.2),
     'L0_xattn_ln_beta': (0.0, 0.1)}
    factors = {}
    for name, (base, spread) in spreads.items():
        noise = np.random.default_rng([zlib.crc32(name.encode()), seed]).standard_normal(out[name].shape)
        drawn = base * np.exp(spread * noise) if base else spread * noise
        out[name] = jnp.asarray(drawn.astype(out[name].dtype))
    for name, factor in factors.items():
        out[name] = (out[name] * factor).astype(out[name].dtype)
    return out
```

```python
from contextlib import ExitStack

import numpy as np

import concourse.bass as bass
from concourse import mybir

ALU = mybir.AluOpType
ACT = mybir.ActivationFunctionType
AX = mybir.AxisListType
F32 = mybir.dt.float32
F32R = mybir.dt.float32r
I32 = mybir.dt.int32
U8 = mybir.dt.uint8

P = 128
NH = 16
E = 8
EPS = 1e-5
RES_SCALE_MAX = 0.3
CLIP = 50.0
LIM = 10000.0
FLT_MAX = float(np.finfo(np.float32).max)
FLT_MIN = float(np.finfo(np.float32).tiny)

MM_USES = ["Q0", "Q1", "W0", "W1", "Q2", "W2", "W3", "Q3", "U0", "U1", "U2", "U3"]
T_USES = ["h0", "h1", "h2", "h3", "c0", "c1", "c2", "c3", "n0", "n1", "n2", "n3", "a0", "a1"]
V_USES = ["v00", "v10", "v20", "v30", "v01", "v11", "v21", "v31", "f0", "f1"]
NEXT = ("Q", "h")
MM_BEFORE = ["Q0", "Q1", "Q2", "Q3", "K0", "K1", "K2", "K3", "V0", "V1"]
T_BEFORE = ["h0", "h1", "h2", "h3"]


def build(nc, x, ctx_t, mask_t, wq_t, bq, wk_t, bk, wv_t, bv, wo_t, bo, gamma, beta, rs, router_t, down_t, up_t, out):
    B, S, H = x.shape
    T = ctx_t.shape[1] // B
    HD = H // NH
    EI = up_t.shape[0]
    EXP_I = EI // E
    KC = H // P
    NT = S // P
    NP = NH // 2
    VW = 2 * HD + 2
    FW = EI + E
    SCALE = 1.0 / float(np.sqrt(HD))
    EXP_HI = float(np.exp(np.float64(CLIP)))
    EXP_LO = float(np.exp(np.float64(-CLIP)))
    ONE = 1.0 + 1e-8
    assert T * 2 == P and H % P == 0 and S == NT * P and HD == 32 and NT == 4 and EI == P

    def ring(uses, before, b, use, last):
        if b is None:
            return before.index(use)
        order = [u for u in uses if not (last and u[0] in NEXT)]
        return len(before) + len(uses) * b + order.index(use)

    def bank(uses, before, b, use, last):
        if b is None:
            return before.index(use) % 2
        order = [u for u in uses if not (last and u[0] in NEXT)]
        return (len(before) + order.index(use)) % 2

    def mm(b, use, last=False):
        return ring(MM_USES, MM_BEFORE, b, use, last), bank(MM_USES, MM_BEFORE, b, use, last)

    def tr(b, use, last=False):
        return ring(T_USES, T_BEFORE, b, use, last), bank(T_USES, T_BEFORE, b, use, last)

    def vr(b, use):
        return len(V_USES) * b + V_USES.index(use), V_USES.index(use) % 2

    stack = ExitStack()
    with stack:
        def sb(name, shape, dt=F32):
            return stack.enter_context(nc.sbuf_tensor(name, shape, dt))

        def sem(name):
            return stack.enter_context(nc.semaphore(name))

        def split(name, shape):
            return sb(name + "_hi", shape, F32R), sb(name + "_lo", shape, F32R)

        xs = sb("xs", [P, B * NT, H])
        stage = sb("stage", [P, 2 * KC, H])
        wq_raw, wo_raw, probs = stage[:, 0:KC, :], stage[:, KC:, :], stage[:, :, :]
        wk = sb("wk", [P, KC, H])
        att, x1n = wk, wk
        wv = sb("wv", [P, KC, H])
        hs, cen = wv, wv
        ctx_sb = wo_raw[:, 0:2, :].rearrange("p a n -> p (a n)").rearrange("p (k n) -> p k n", k=KC)
        wq_hi, wq_lo = split("wq", [P, KC, H])
        wo_hi, wo_lo = split("wo", [P, KC, H])
        dr_raw = sb("dr_raw", [P, KC, FW])
        dr_hi, dr_lo = split("dr", [P, KC, FW])
        up_raw = sb("up_raw", [EI, H])
        up_hi, up_lo = split("up", [EI, H])
        compare = sb("compare", [P, 4, NT * E * E])
        ctx_clean = compare[:, :, :]
        ctx_notnan = sb("ctx_notnan", [P, KC, B * T], U8)
        ctx_finite = sb("ctx_finite", [P, KC, B * T], U8)
        k_hl = sb("k_hl", [P, 2, KC, B * T], F32R)
        kbd = sb("kbd", [P, 2 * KC, 2 * T], F32R)
        vbd = sb("vbd", [P, B, NP, VW])
        q_hi, q_lo = split("q", [P, KC, S])
        hst_hi, hst_lo = split("hst", [P, NT, KC, P])
        attt_hi, attt_lo = split("attt", [P, NT, KC, P])
        x1t_hi, x1t_lo = attt_hi, attt_lo
        hidden = sb("hidden", [P, 3 * NT, EI])
        hid_tanh, hid, hidg = (hidden[:, i * NT:(i + 1) * NT, :] for i in range(3))
        hid_out = hidden[:, 2 * NT:, :].rearrange("p t n -> p (t n)")
        ctx_lim = hidden[:, 0:2 * NT, :].rearrange("p t n -> p (t n)").rearrange("p (k n) -> p k n", k=KC)
        hidt_hi, hidt_lo = split("hidt", [EI, NT, P])

        ident = sb("ident", [P, P])
        least = sb("least", [P, E, E])
        ones_k = sb("ones_k", [33, P], F32R)
        ones_f = sb("ones_f", [33, P])
        bo_raw = hid_out[0:33, :]
        bo_hl = sb("bo_hl", [33, H], F32R)
        bo_hi32 = sb("bo_hi32", [33, H], F32R)
        gamma_bc = sb("gamma_bc", [P, H])
        gamma_rs = gamma_bc
        beta_bc = sb("beta_bc", [P, H])
        bv_bc = sb("bv_bc", [P, H])
        bq_sb = sb("bq_sb", [P, KC])
        bk_sb = sb("bk_sb", [P, KC])
        rs_raw = sb("rs_raw", [P, 1])
        rs_sb = sb("rs_sb", [P, 1])
        rs_sq = sb("rs_sq", [P, 1])
        mask_sb = sb("mask_sb", [P, B], I32)
        attend = sb("attend", [P, B])
        exp_max = sb("exp_max", [P, B])
        exp_min = sb("exp_min", [P, 1])
        eps_sb = sb("eps_sb", [P, 1])
        minus_half = sb("minus_half", [P, NT])

        ln_st = sb("ln_st", [P, NT, 6])
        ln_mv = sb("ln_mv", [P, NT, 2])
        ln_ve = sb("ln_ve", [P, NT])
        ln_nm = sb("ln_nm", [P, NT])
        ln_rstd = sb("ln_rstd", [P, NT])
        ln_bias = sb("ln_bias", [P, NT])
        d_st = sb("d_st", [P, NT, 6])
        d_mv = sb("d_mv", [P, NT, 2])
        d_ve = sb("d_ve", [P, NT])
        d_rstd = sb("d_rstd", [P, NT])
        n_st = sb("n_st", [P, NT, 6])
        n_mv = sb("n_mv", [P, NT, 2])
        n_ve = sb("n_ve", [P, NT])
        n_rstd = sb("n_rstd", [P, NT])
        rz = sb("rz", [P, NT, 2, 4, 2])
        lg = sb("lg", [P, NT, E])
        lmax = sb("lmax", [P, NT])
        lsub = sb("lsub", [P, NT, E])
        lexp = sb("lexp", [P, NT, E])
        diff, beats = (compare[:, i, :].rearrange("p (t e f) -> p t e f", t=NT, e=E) for i in range(2))
        rank = sb("rank", [P, NT, E])
        kept = sb("kept", [P, NT, E])
        lsum = sb("lsum", [P, NT])
        lrec = sb("lrec", [P, NT])
        gate = sb("gate", [P, NT, E])

        def banks(name):
            return [stack.enter_context(nc.psum_tensor(f"{name}{i}", [P, 512], F32)) for i in range(2)]

        ps_mm, ps_t, ps_s, ps_v = banks("ps_mm"), banks("ps_t"), banks("ps_s"), banks("ps_v")

        x0_in, xr_in, ctx_in, wq_in, wk_in, wv_in, wo_in, ffn_in, small_in, mask_in = [
            sem(n) for n in ("x0_in", "xr_in", "ctx_in", "wq_in", "wk_in", "wv_in", "wo_in", "ffn_in", "small_in",
                             "mask_in")]
        stored = sem("stored")
        mm_full, mm_free, t_full, t_free = sem("mm_full"), sem("mm_free"), sem("t_full"), sem("t_free")
        s_full, v_full, v_free = sem("s_full"), sem("v_full"), sem("v_free")
        zeroed, ident_ok, half_ok, least_ok, ones_ok = (
            sem("zeroed"), sem("ident_ok"), sem("half_ok"), sem("least_ok"), sem("ones_ok"))
        bo_step, rs_step, mask_step, vones_ok, gamma_ok = (
            sem("bo_step"), sem("rs_step"), sem("mask_step"), sem("vones_ok"), sem("gamma_ok"))
        ctx_part, ctx_ok = sem("ctx_part"), sem("ctx_ok")
        wq_hi_ok, wq_lo_ok, wo_hi_ok, wo_lo_ok, ffn_hi_ok, ffn_lo_ok = [
            sem(n) for n in ("wq_hi_ok", "wq_lo_ok", "wo_hi_ok", "wo_lo_ok", "ffn_hi_ok", "ffn_lo_ok")]
        k_hi_ok, k_ok, v_ok, kbd_ok = sem("k_hi_ok"), sem("k_ok"), sem("v_ok"), sem("kbd_ok")
        ln_st_ok, ln_mv_ok, ln_ve_ok, ln_rstd_ok, hs_ok = (
            sem("ln_st_ok"), sem("ln_mv_ok"), sem("ln_ve_ok"), sem("ln_rstd_ok"), sem("hs_ok"))
        hst_hi_ok, q_hi_ok = sem("hst_hi_ok"), sem("q_hi_ok")
        exp_ok, probs_ok = sem("exp_ok"), sem("probs_ok")
        rz_ok = sem("rz_ok")
        attt_hi_ok = sem("attt_hi_ok")
        xb_ok = sem("xb_ok")
        d_st_ok, d_mv_ok, d_ve_ok, d_rstd_ok, cen_ok, x1_ok = (
            sem("d_st_ok"), sem("d_mv_ok"), sem("d_ve_ok"), sem("d_rstd_ok"), sem("cen_ok"), sem("x1_ok"))
        n_st_ok, n_mv_ok, n_ve_ok, n_rstd_ok, x1n_ok, x1t_hi_ok = (
            sem("n_st_ok"), sem("n_mv_ok"), sem("n_ve_ok"), sem("n_rstd_ok"), sem("x1n_ok"), sem("x1t_hi_ok"))
        tanh_ok, lg_ok, lmax_ok, lsub_ok, lexp_ok = (
            sem("tanh_ok"), sem("lg_ok"), sem("lmax_ok"), sem("lsub_ok"), sem("lexp_ok"))
        diff_ok, beats_ok, rank_ok, kept_ok, lsum_ok, lrec_ok, gate_ok, hid_ok, hidg_ok, hidt_hi_ok = [
            sem(n) for n in ("diff_ok", "beats_ok", "rank_ok", "kept_ok", "lsum_ok", "lrec_ok", "gate_ok",
                             "hid_ok", "hidg_ok", "hidt_hi_ok")]

        block = stack.enter_context(nc.Block())

        def wide(w):
            return w.rearrange("(k p) n -> p k n", p=P)

        x_tiles = x.rearrange("b (t p) h -> p (b t) h", p=P)
        out_tiles = out.rearrange("b (t p) h -> p (b t) h", p=P)
        SMALL = 16 * 8

        @block.sync
        def _(sp):
            for t in range(NT):
                sp.dma_start(xs[:, t, :], x_tiles[:, t, :]).then_inc(x0_in, 16)
            sp.dma_start(wq_raw[:, :, :], wide(wq_t)).then_inc(wq_in, 16)
            sp.dma_start(ctx_sb[:, :, :], wide(ctx_t)).then_inc(ctx_in, 16)
            sp.dma_start(wk[:, :, :], wide(wk_t)).then_inc(wk_in, 16)
            sp.dma_start(xs[:, NT:, :], x_tiles[:, NT:, :]).then_inc(xr_in, 16)
            sp.wait_ge(t_full, NT)
            sp.dma_start(wv[:, :, :], wide(wv_t)).then_inc(wv_in, 16)
            sp.wait_ge(ctx_ok, 1)
            sp.dma_start(wo_raw[:, :, :], wide(wo_t)).then_inc(wo_in, 16)
            sp.dma_start(dr_raw[:, :, 0:EI], wide(down_t)).then_inc(ffn_in, 16)
            sp.dma_start(dr_raw[:, :, EI:FW], wide(router_t)).then_inc(ffn_in, 16)
            sp.dma_start(up_raw[:, :], up_t).then_inc(ffn_in, 16)

            def store(b, last=False):
                for t in range(NT):
                    sp.wait_ge(mm_free, mm(b, f"U{t}", last)[0] + 1)
                    sp.dma_start(out_tiles[:, bass.ds(NT * b + t, 1), :],
                                 xs[:, bass.ds(NT * b + t, 1), :]).then_inc(stored, 16)

            with sp.Fori(0, B - 1, 1) as b:
                store(b)
            store(B - 1, last=True)
            sp.wait_ge(stored, 16 * B * NT)

        def rows(v, n):
            return v.rearrange("(a h) -> a h", a=1).broadcast_to([n, H])

        @block.tensor
        def _(pe):
            def passes(dst, pairs, start=True, stop=True):
                n = len(pairs)
                for i, (w, m) in enumerate(pairs):
                    last = pe.matmul(dst, w, m, start=start and i == 0, stop=stop and i == n - 1)
                return last

            def three(hi_w, lo_w, hi_m, lo_m):
                return [(hi_w, hi_m), (hi_w, lo_m), (lo_w, hi_m)]

            def take(use, free):
                u, k = use
                if isinstance(u, int) and u < 2:
                    return k
                pe.wait_ge(free, u - 1)
                return k

            def hs_transpose(bb, b, t, last=False):
                pe.wait_ge(hs_ok, NT * bb + t + 1)
                k = take(tr(b, f"h{t}"), t_free)
                for c in range(KC):
                    mmi = pe.transpose(ps_t[k][:, c * P:(c + 1) * P], hs[:, t, c * P:(c + 1) * P], ident[:, :])
                mmi.then_inc(t_full, 1)

            def query(bb, b, m):
                k = take(mm(b, f"Q{m}"), mm_free)
                if m == 0:
                    pe.wait_ge(t_free, tr(b, "h3")[0] + 1)
                pairs = []
                for c in range(KC):
                    cols = slice(m * P, (m + 1) * P)
                    pairs += three(wq_hi[:, c, cols], wq_lo[:, c, cols], hst_hi[:, :, c, :], hst_lo[:, :, c, :])
                passes(ps_mm[k][:, :], pairs).then_inc(mm_full, 1)

            def keys(m):
                k = take(mm(None, f"K{m}"), mm_free)
                passes(ps_mm[k][:, 0:B * T], [(wk[:, c, m * P:(m + 1) * P], ctx_clean[:, c, :]) for c in range(KC)]
                       ).then_inc(mm_full, 1)

            def values(j):
                k = take(mm(None, f"V{j}"), mm_free)
                passes(ps_mm[k][:, :], [(ctx_clean[:, c, j * P:(j + 1) * P], wv[:, c, :]) for c in range(KC)]
                       ).then_inc(mm_full, 1)

            def scores(b, p, first):
                if not first or p >= 2:
                    pe.wait_ge(exp_ok, NP * b + p - 1)
                if p == 0:
                    pe.wait_ge(kbd_ok, 4 * (b + 1))
                c, r = p // 2, slice(64 * (p % 2), 64 * (p % 2) + 64)
                passes(ps_s[p % 2][:, :],
                       three(kbd[r, c, :], kbd[r, KC + c, :], q_hi[r, c, :], q_lo[r, c, :])).then_inc(s_full, 1)

            def weigh(b, t, g):
                u, k = vr(b, f"v{t}{g}")
                if not (isinstance(b, int) and u < 2):
                    pe.wait_ge(v_free, u - 1)
                if t == 0:
                    pe.wait_ge(probs_ok, NP * b + 4 * g + 4)
                for i in range(4):
                    p = 4 * g + i
                    mmi = pe.matmul(ps_v[k][:, i * VW:(i + 1) * VW], probs[:, p, t * P:(t + 1) * P],
                                    vbd[:, b, p, :], start=True, stop=True)
                mmi.then_inc(v_full, 1)

            def att_transpose(b, t, last):
                pe.wait_ge(v_free, vr(b, f"v{t}1")[0] + 1)
                k = take(tr(b, f"c{t}", last), t_free)
                for c in range(KC):
                    mmi = pe.transpose(ps_t[k][:, c * P:(c + 1) * P], att[:, t, c * P:(c + 1) * P], ident[:, :])
                mmi.then_inc(t_full, 1)

            def project(b, t, last):
                pe.wait_ge(t_free, tr(b, f"c{t}", last)[0] + 1)
                k = take(mm(b, f"W{t}", last), mm_free)
                pairs = [(ones_k[:, :], bo_hl[:, :])]
                for c in range(KC):
                    pairs += three(attt_hi[:, t, c, :], attt_lo[:, t, c, :], wo_hi[:, c, :], wo_lo[:, c, :])
                passes(ps_mm[k][:, :], pairs).then_inc(mm_full, 1)

            def x1n_transpose(b, t, last):
                pe.wait_ge(x1n_ok, NT * b + t + 1)
                k = take(tr(b, f"n{t}", last), t_free)
                for c in range(KC):
                    mmi = pe.transpose(ps_t[k][:, c * P:(c + 1) * P], x1n[:, t, c * P:(c + 1) * P], ident[:, :])
                mmi.then_inc(t_full, 1)

            def down(b, j, last):
                u, k = vr(b, f"f{j}")
                pe.wait_ge(v_free, u - 1)
                for i in range(2):
                    t = 2 * j + i
                    pe.wait_ge(t_free, tr(b, f"n{t}", last)[0] + 1)
                    pairs = []
                    for c in range(KC):
                        pairs += three(x1t_hi[:, t, c, :], x1t_lo[:, t, c, :], dr_hi[:, c, :], dr_lo[:, c, :])
                    mmi = passes(ps_v[k][:, i * FW:(i + 1) * FW], pairs)
                mmi.then_inc(v_full, 1)

            def hid_transpose(b, j, last):
                pe.wait_ge(hidg_ok, 2 * b + j + 1)
                k = take(tr(b, f"a{j}", last), t_free)
                for i in range(2):
                    mmi = pe.transpose(ps_t[k][:, i * P:(i + 1) * P], hidg[:, 2 * j + i, :], ident[:, :])
                mmi.then_inc(t_full, 1)

            def up(b, t, last):
                if t % 2 == 0:
                    pe.wait_ge(t_free, tr(b, f"a{t // 2}", last)[0] + 1)
                k = take(mm(b, f"U{t}", last), mm_free)
                passes(ps_mm[k][:, :], three(hidt_hi[:, t, :], hidt_lo[:, t, :], up_hi[:, :], up_lo[:, :])
                       ).then_inc(mm_full, 1)

            def step(b, first=False, last=False):
                nb = None if last else b + 1
                if first:
                    pe.wait_ge(mm_free, len(MM_BEFORE))
                else:
                    pe.wait_ge(mm_free, mm(b - 1, "Q3")[0] + 1)
                for p in range(NP):
                    scores(b, p, first)
                for t in (0, 1):
                    if not last:
                        hs_transpose(nb, b, t)
                weigh(b, 0, 0)
                weigh(b, 1, 0)
                for t in (2, 3):
                    if not last:
                        hs_transpose(nb, b, t)
                weigh(b, 2, 0)
                weigh(b, 3, 0)
                for t in range(NT):
                    weigh(b, t, 1)
                if not last:
                    query(nb, b, 0)
                att_transpose(b, 0, last)
                att_transpose(b, 1, last)
                if not last:
                    query(nb, b, 1)
                att_transpose(b, 2, last)
                att_transpose(b, 3, last)
                project(b, 0, last)
                project(b, 1, last)
                if not last:
                    query(nb, b, 2)
                project(b, 2, last)
                project(b, 3, last)
                x1n_transpose(b, 0, last)
                x1n_transpose(b, 1, last)
                down(b, 0, last)
                if not last:
                    query(nb, b, 3)
                x1n_transpose(b, 2, last)
                x1n_transpose(b, 3, last)
                down(b, 1, last)
                hid_transpose(b, 0, last)
                up(b, 0, last)
                up(b, 1, last)
                hid_transpose(b, 1, last)
                up(b, 2, last)
                up(b, 3, last)

            pe.wait_ge(ident_ok, 1)
            for t in range(NT):
                hs_transpose(0, None, t)
            pe.wait_ge(wq_hi_ok, KC)
            pe.wait_ge(wq_lo_ok, KC)
            for m in range(KC):
                query(0, None, m)
            pe.wait_ge(ctx_ok, 1)
            pe.wait_ge(wk_in, 16)
            for m in range(KC):
                keys(m)
            pe.wait_ge(wv_in, 16)
            for j in range(2):
                values(j)
            pe.wait_ge(wo_hi_ok, KC)
            pe.wait_ge(wo_lo_ok, KC)
            pe.wait_ge(bo_step, 3)
            pe.wait_ge(ones_ok, 1)
            pe.wait_ge(ffn_hi_ok, 2)
            pe.wait_ge(ffn_lo_ok, 2)
            step(0, first=True)
            with pe.Fori(1, B - 1, 1) as b:
                step(b)
            step(B - 1, last=True)

        @block.scalar
        def _(act):
            def hs_hi(b, t):
                u, k = tr(b, f"h{t}")
                act.wait_ge(t_full, u + 1)
                act.copy(hst_hi[:, t, :, :], ps_t[k][:, :].rearrange("p (c n) -> p c n", c=KC)).then_inc(hst_hi_ok, 1)

            def query_hi(b, m):
                u, k = mm(b, f"Q{m}")
                act.wait_ge(mm_full, u + 1)
                act.activation(q_hi[:, m, :], ps_mm[k][:, :], ACT.Identity, bias=bq_sb[:, m:m + 1]).then_inc(q_hi_ok, 1)

            def key_hi(m):
                u, k = mm(None, f"K{m}")
                act.wait_ge(mm_full, u + 1)
                act.activation(k_hl[:, 0, m, :], ps_mm[k][:, 0:B * T], ACT.Identity, bias=bk_sb[:, m:m + 1]
                               ).then_inc(k_hi_ok, 1)

            def hs_norm(bb, t):
                act.wait_ge(ln_rstd_ok, 2 * bb + 2)
                act.activation(hs[:, t, :], xs[:, NT * bb + t, :], ACT.Identity, bias=ln_bias[:, t:t + 1],
                               scale=ln_rstd[:, t:t + 1]).then_inc(hs_ok, 1)

            def exp_scores(b, p):
                act.wait_ge(s_full, NP * b + p + 1)
                act.activation(probs[:, p, :], ps_s[p % 2][:, :], ACT.Exp, scale=SCALE).then_inc(exp_ok, 1)

            def att_hi(b, t, last):
                u, k = tr(b, f"c{t}", last)
                act.wait_ge(t_full, u + 1)
                act.copy(attt_hi[:, t, :, :], ps_t[k][:, :].rearrange("p (c n) -> p c n", c=KC)).then_inc(attt_hi_ok, 1)

            def x1_hi(b, t, last):
                u, k = tr(b, f"n{t}", last)
                act.wait_ge(t_full, u + 1)
                act.copy(x1t_hi[:, t, :, :], ps_t[k][:, :].rearrange("p (c n) -> p c n", c=KC)).then_inc(x1t_hi_ok, 1)

            def gates(b, j):
                u, k = vr(b, f"f{j}")
                act.wait_ge(v_full, u + 1)
                act.activation(hid_tanh[:, 2 * j:2 * j + 2, :],
                               ps_v[k][:, 0:2 * FW].rearrange("p (i f) -> p i f", i=2)[:, :, 0:EI],
                               ACT.Tanh, scale=0.5).then_inc(tanh_ok, 1)
                act.wait_ge(lsub_ok, 2 * b + j + 1)
                act.activation(lexp[:, 2 * j:2 * j + 2, :], lsub[:, 2 * j:2 * j + 2, :], ACT.Exp).then_inc(lexp_ok, 1)

            def hid_hi(b, j, last):
                u, k = tr(b, f"a{j}", last)
                act.wait_ge(t_full, u + 1)
                act.copy(hidt_hi[:, 2 * j:2 * j + 2, :], ps_t[k][:, 0:2 * P].rearrange("p (i n) -> p i n", i=2)
                         ).then_inc(hidt_hi_ok, 1)

            def step(b, last=False):
                for p in range(NP):
                    exp_scores(b, p)
                    if 3 <= p < 3 + NT and not last:
                        hs_norm(b + 1, p - 3)
                if not last:
                    for t in range(NT):
                        hs_hi(b, t)
                    query_hi(b, 0)
                att_hi(b, 0, last)
                att_hi(b, 1, last)
                if not last:
                    query_hi(b, 1)
                att_hi(b, 2, last)
                att_hi(b, 3, last)
                if not last:
                    query_hi(b, 2)
                x1_hi(b, 0, last)
                x1_hi(b, 1, last)
                gates(b, 0)
                if not last:
                    query_hi(b, 3)
                x1_hi(b, 2, last)
                x1_hi(b, 3, last)
                gates(b, 1)
                hid_hi(b, 0, last)
                hid_hi(b, 1, last)

            act.dma_start(bq_sb[:, :], bq).then_inc(small_in, 16)
            act.dma_start(bk_sb[:, :], bk).then_inc(small_in, 16)
            act.dma_start(rs_raw[:, :], rs.broadcast_to([P, 1])).then_inc(small_in, 16)
            act.dma_start(bo_raw[0:1, :], rows(bo, 1)).then_inc(small_in, 16)
            act.dma_start(bo_raw[32:33, :], rows(bo, 1)).then_inc(small_in, 16)
            for half in range(2):
                act.dma_start(mask_sb[half * T:(half + 1) * T, :], mask_t).then_inc(mask_in, 16)
            act.dma_start(gamma_bc[:, :], rows(gamma, P)).then_inc(small_in, 16)
            act.dma_start(beta_bc[:, :], rows(beta, P)).then_inc(small_in, 16)
            act.dma_start(bv_bc[:, :], rows(bv, P)).then_inc(small_in, 16)
            for t in range(NT):
                hs_norm(0, t)
            act.wait_ge(wq_in, 16)
            for c in range(KC):
                act.copy(wq_hi[:, c, :], wq_raw[:, c, :]).then_inc(wq_hi_ok, 1)
            for t in range(NT):
                hs_hi(None, t)
            act.wait_ge(small_in, SMALL)
            for m in range(KC):
                query_hi(None, m)
            for m in range(KC):
                key_hi(m)
            act.wait_ge(wo_in, 16)
            for c in range(KC):
                act.copy(wo_hi[:, c, :], wo_raw[:, c, :]).then_inc(wo_hi_ok, 1)
            act.wait_ge(ffn_in, 48)
            act.copy(dr_hi[:, :, :], dr_raw[:, :, :]).then_inc(ffn_hi_ok, 1)
            act.copy(up_hi[:, :], up_raw[:, :]).then_inc(ffn_hi_ok, 1)
            act.wait_ge(wq_lo_ok, KC)
            act.wait_ge(wo_lo_ok, KC)
            with act.Fori(0, B - 1, 1) as b:
                step(b)
            step(B - 1, last=True)

        @block.vector
        def _(dve):
            def hold(semaphore, value):
                dve.wait_ge(semaphore, value)
                dve.nop(nofuse=True)

            def ln_stats(bb):
                for t in range(NT):
                    if isinstance(bb, int) and bb == 0:
                        dve.wait_ge(x0_in, 16 * NT)
                    dve.bn_stats(ln_st[:, t, :], xs[:, NT * bb + t, :]).then_inc(ln_st_ok, 1)
                for t in range(NT):
                    hold(ln_st_ok, NT * bb + t + 1)
                    dve.bn_aggr(ln_mv[:, t, :], ln_st[:, t, :]).then_inc(ln_mv_ok, 1)
                dve.wait_ge(ln_mv_ok, NT * bb + NT)
                dve.tensor_scalar(ln_ve[:, :], ln_mv[:, :, 1], EPS, None, ALU.add).then_inc(ln_ve_ok, 1)
                dve.tensor_scalar(ln_nm[:, :], ln_mv[:, :, 0], -1.0, None, ALU.mult).then_inc(ln_ve_ok, 1)

            def lo_of_bank(dst, hi, k, width, parts):
                src = ps_t[k][:, 0:width * P].rearrange("p (c n) -> p c n", c=width)
                return dve.tensor_tensor(dst, src, hi.bitcast(F32), ALU.subtract)

            def hs_lo(b, t):
                u, k = tr(b, f"h{t}")
                dve.wait_ge(hst_hi_ok, (0 if b is None else NT * (b + 1)) + t + 1)
                lo_of_bank(hst_lo[:, t, :, :], hst_hi[:, t, :, :], k, KC, P).then_inc(t_free, 1)

            def query_lo(b, m):
                u, k = mm(b, f"Q{m}")
                dve.wait_ge(q_hi_ok, (0 if b is None else KC * (b + 1)) + m + 1)
                dve.scalar_tensor_tensor(q_lo[:, m, :], ps_mm[k][:, :], bq_sb[:, m:m + 1], q_hi[:, m, :].bitcast(F32),
                                         ALU.add, ALU.subtract).then_inc(mm_free, 1)

            def key_lo(m):
                u, k = mm(None, f"K{m}")
                dve.wait_ge(k_hi_ok, m + 1)
                dve.scalar_tensor_tensor(k_hl[:, 1, m, :], ps_mm[k][:, 0:B * T], bk_sb[:, m:m + 1],
                                         k_hl[:, 0, m, :].bitcast(F32), ALU.add, ALU.subtract
                                         ).then_inc(mm_free, 1)

            def value_blocks(j):
                u, k = mm(None, f"V{j}")
                dve.wait_ge(mm_full, u + 1)
                for i in range(2):
                    for s in range(2):
                        rows_in, rows_out = slice(i * T, (i + 1) * T), slice(s * T, (s + 1) * T)
                        src = ps_mm[k][rows_in, :].rearrange("p (n s d) -> p n s d", s=2, d=HD)[:, :, s, :]
                        bias = bv_bc[rows_in, :].rearrange("p (n s d) -> p n s d", s=2, d=HD)[:, :, s, :]
                        final = (i, s) == (1, 1)
                        if final:
                            dve.wait_ge(v_ok, 3 * (j + 1))
                        dve.tensor_tensor(vbd[rows_out, 2 * j + i, :, s * HD:(s + 1) * HD], src, bias, ALU.add
                                          ).then_inc(mm_free if final else v_ok, 1)

            def clip(b, p):
                dve.wait_ge(exp_ok, NP * b + p + 1)
                dve.tensor_scalar(probs[:, p, :], probs[:, p, :], exp_min[:, 0:1], exp_max[:, bass.ds(b, 1)],
                                  ALU.max, ALU.min).then_inc(probs_ok, 1)

            def normalise(b, t, g):
                u, k = vr(b, f"v{t}{g}")
                v = ps_v[k][:, 0:4 * VW].rearrange("p (n w) -> p n w", n=4)
                dve.wait_ge(v_full, u + 1)
                dve.reciprocal(rz[:, t, g, :, :], v[:, :, 2 * HD:VW]).then_inc(rz_ok, 1)
                dve.wait_ge(rz_ok, 8 * b + V_USES.index(f"v{t}{g}") + 1)
                dve.tensor_tensor(att[:, t, 4 * 2 * HD * g:4 * 2 * HD * (g + 1)].rearrange(
                                      "p (n s d) -> p n s d", n=4, s=2),
                                  v[:, :, 0:2 * HD].rearrange("p n (s d) -> p n s d", s=2),
                                  rz[:, t, g, :, :].unsqueeze(3).broadcast_to([P, 4, 2, HD]), ALU.mult
                                  ).then_inc(v_free, 1)

            def att_lo(b, t, last):
                u, k = tr(b, f"c{t}", last)
                dve.wait_ge(attt_hi_ok, NT * b + t + 1)
                lo_of_bank(attt_lo[:, t, :, :], attt_hi[:, t, :, :], k, KC, P).then_inc(t_free, 1)

            def residual(b, t, last):
                u, k = mm(b, f"W{t}", last)
                n = NT * b + t + 1
                hold(mm_full, u + 1)
                dve.bn_stats(d_st[:, t, :], ps_mm[k][:, :]).then_inc(d_st_ok, 1)
                hold(d_st_ok, n)
                dve.bn_aggr(d_mv[:, t, :], d_st[:, t, :]).then_inc(d_mv_ok, 1)
                dve.wait_ge(d_mv_ok, n)
                dve.tensor_scalar(d_ve[:, t:t + 1], d_mv[:, t, 1:2], rs_sq[:, :], eps_sb[:, :], ALU.mult, ALU.add
                                  ).then_inc(d_ve_ok, 1)
                dve.scalar_tensor_tensor(cen[:, t, :], ps_mm[k][:, :], d_mv[:, t, 0:1], gamma_rs[:, :],
                                         ALU.subtract, ALU.mult).then_inc(mm_free, 1)
                dve.wait_ge(mm_free, u + 1)
                dve.wait_ge(d_rstd_ok, n)
                dve.wait_ge(xb_ok, NT * b + NT)
                xt = xs[:, NT * b + t, :]
                dve.scalar_tensor_tensor(xt, cen[:, t, :], d_rstd[:, t:t + 1], xt, ALU.mult, ALU.add
                                         ).then_inc(x1_ok, 1)
                hold(x1_ok, n)
                dve.bn_stats(n_st[:, t, :], xt).then_inc(n_st_ok, 1)
                hold(n_st_ok, n)
                dve.bn_aggr(n_mv[:, t, :], n_st[:, t, :]).then_inc(n_mv_ok, 1)
                dve.wait_ge(n_mv_ok, n)
                dve.tensor_scalar(n_ve[:, t:t + 1], n_mv[:, t, 1:2], EPS, None, ALU.add).then_inc(n_ve_ok, 1)

            def x1_norm(b, t):
                dve.wait_ge(n_rstd_ok, NT * b + t + 1)
                dve.tensor_scalar(x1n[:, t, :], xs[:, NT * b + t, :], n_mv[:, t, 0:1], n_rstd[:, t:t + 1],
                                  ALU.subtract, ALU.mult).then_inc(x1n_ok, 1)

            def x1_lo(b, t, last):
                u, k = tr(b, f"n{t}", last)
                dve.wait_ge(x1t_hi_ok, NT * b + t + 1)
                lo_of_bank(x1t_lo[:, t, :, :], x1t_hi[:, t, :, :], k, KC, P).then_inc(t_free, 1)

            def router(b, j):
                u, k = vr(b, f"f{j}")
                n, ts = 2 * b + j + 1, slice(2 * j, 2 * j + 2)
                f = ps_v[k][:, 0:2 * FW].rearrange("p (i f) -> p i f", i=2)
                dve.wait_ge(tanh_ok, n)
                dve.tensor_copy(lg[:, ts, :], f[:, :, EI:FW]).then_inc(lg_ok, 1)
                dve.scalar_tensor_tensor(hid[:, ts, :], hid_tanh[:, ts, :], 1.0, f[:, :, 0:EI], ALU.add, ALU.mult
                                         ).then_inc(v_free, 1)
                dve.wait_ge(lg_ok, n)
                dve.tensor_reduce(lmax[:, ts], lg[:, ts, :], AX.X, ALU.max).then_inc(lmax_ok, 1)
                dve.wait_ge(lmax_ok, n)
                dve.tensor_tensor(lsub[:, ts, :], lg[:, ts, :], lmax[:, ts].unsqueeze(2).broadcast_to([P, 2, E]),
                                  ALU.subtract).then_inc(lsub_ok, 1)

            def gating(b, j):
                n, ts = 2 * b + j + 1, slice(2 * j, 2 * j + 2)
                dve.wait_ge(lexp_ok, n)
                dve.tensor_reduce(lsum[:, ts], lexp[:, ts, :], AX.X, ALU.add).then_inc(lsum_ok, 1)
                dve.wait_ge(lsum_ok, n)
                dve.reciprocal(lrec[:, ts], lsum[:, ts]).then_inc(lrec_ok, 1)
                dve.wait_ge(diff_ok, n)
                dve.tensor_tensor(beats[:, ts, :, :], diff[:, ts, :, :],
                                  least[:, :, :].unsqueeze(1).broadcast_to([P, 2, E, E]), ALU.is_gt
                                  ).then_inc(beats_ok, 1)
                dve.wait_ge(beats_ok, n)
                dve.tensor_reduce(rank[:, ts, :], beats[:, ts, :, :], AX.X, ALU.add).then_inc(rank_ok, 1)
                dve.wait_ge(rank_ok, n)
                dve.scalar_tensor_tensor(kept[:, ts, :], rank[:, ts, :], 1.5, lexp[:, ts, :], ALU.is_lt, ALU.mult
                                         ).then_inc(kept_ok, 1)
                dve.wait_ge(kept_ok, n)
                dve.wait_ge(lrec_ok, n)
                dve.scalar_tensor_tensor(gate[:, ts, :], kept[:, ts, :], 0.5,
                                         lrec[:, ts].unsqueeze(2).broadcast_to([P, 2, E]), ALU.mult, ALU.mult
                                         ).then_inc(gate_ok, 1)
                dve.wait_ge(gate_ok, n)
                dve.wait_ge(v_free, vr(b, f"f{j}")[0] + 1)
                dve.tensor_tensor(hidg[:, ts, :].rearrange("p t (e i) -> p t e i", e=E),
                                  hid[:, ts, :].rearrange("p t (e i) -> p t e i", e=E),
                                  gate[:, ts, :].unsqueeze(3).broadcast_to([P, 2, E, EXP_I]), ALU.mult
                                  ).then_inc(hidg_ok, 1)

            def hid_lo(b, j, last):
                u, k = tr(b, f"a{j}", last)
                dve.wait_ge(hidt_hi_ok, 2 * b + j + 1)
                lo_of_bank(hidt_lo[:, 2 * j:2 * j + 2, :], hidt_hi[:, 2 * j:2 * j + 2, :], k, 2, P).then_inc(t_free, 1)

            def finish(b, t, last):
                u, k = mm(b, f"U{t}", last)
                dve.wait_ge(mm_full, u + 1)
                xt = xs[:, NT * b + t, :]
                dve.tensor_tensor(xt, ps_mm[k][:, :], xt, ALU.add).then_inc(mm_free, 1)

            def step(b, last=False):
                if not last:
                    ln_stats(b + 1)
                for p in range(NP):
                    clip(b, p)
                if not last:
                    hs_lo(b, 0)
                    hs_lo(b, 1)
                normalise(b, 0, 0)
                normalise(b, 1, 0)
                if not last:
                    hs_lo(b, 2)
                    hs_lo(b, 3)
                normalise(b, 2, 0)
                normalise(b, 3, 0)
                for t in range(NT):
                    normalise(b, t, 1)
                if not last:
                    query_lo(b, 0)
                att_lo(b, 0, last)
                att_lo(b, 1, last)
                if not last:
                    query_lo(b, 1)
                att_lo(b, 2, last)
                att_lo(b, 3, last)
                residual(b, 0, last)
                residual(b, 1, last)
                x1_norm(b, 0)
                if not last:
                    query_lo(b, 2)
                residual(b, 2, last)
                x1_norm(b, 1)
                residual(b, 3, last)
                x1_norm(b, 2)
                x1_norm(b, 3)
                x1_lo(b, 0, last)
                x1_lo(b, 1, last)
                router(b, 0)
                gating(b, 0)
                if not last:
                    query_lo(b, 3)
                x1_lo(b, 2, last)
                x1_lo(b, 3, last)
                router(b, 1)
                gating(b, 1)
                hid_lo(b, 0, last)
                finish(b, 0, last)
                finish(b, 1, last)
                hid_lo(b, 1, last)
                finish(b, 2, last)
                finish(b, 3, last)

            dve.memset(exp_min[:, :], EXP_LO).then_inc(rs_step, 1)
            dve.memset(eps_sb[:, :], EPS).then_inc(rs_step, 1)
            ln_stats(0)
            dve.wait_ge(wq_in, 16)
            for c in range(KC):
                dve.wait_ge(wq_hi_ok, c + 1)
                dve.tensor_tensor(wq_lo[:, c, :], wq_raw[:, c, :], wq_hi[:, c, :].bitcast(F32), ALU.subtract
                                  ).then_inc(wq_lo_ok, 1)
            for t in range(NT):
                hs_lo(None, t)
            dve.wait_ge(ctx_in, 16)
            dve.tensor_scalar(ctx_lim[:, :, :], ctx_sb[:, :, :], -LIM, LIM, ALU.max, ALU.min).then_inc(ctx_part, 1)
            dve.tensor_tensor(ctx_notnan[:, :, :], ctx_sb[:, :, :], ctx_sb[:, :, :], ALU.is_equal
                              ).then_inc(ctx_part, 1)
            dve.wait_ge(small_in, SMALL)
            query_lo(None, 0)
            dve.tensor_scalar(ctx_finite[:, :, :], ctx_sb[:, :, :], 0.0, 0.0, ALU.mult, ALU.is_equal
                              ).then_inc(ctx_part, 1)
            dve.wait_ge(zeroed, 3)
            dve.wait_ge(ctx_part, 3)
            dve.copy_predicated(ctx_clean[:, :, :], ctx_notnan[:, :, :], ctx_lim[:, :, :]).then_inc(ctx_part, 1)
            query_lo(None, 1)
            dve.wait_ge(ctx_part, 4)
            dve.copy_predicated(ctx_clean[:, :, :], ctx_finite[:, :, :], ctx_sb[:, :, :]).then_inc(ctx_ok, 1)
            query_lo(None, 2)
            dve.tensor_scalar(rs_sb[:, :], rs_raw[:, :], 0.0, RES_SCALE_MAX, ALU.max, ALU.min).then_inc(rs_step, 1)
            dve.wait_ge(rs_step, 3)
            dve.tensor_scalar(rs_sq[:, :], rs_sb[:, :], rs_sb[:, :], None, ALU.mult).then_inc(rs_step, 1)
            dve.tensor_scalar(gamma_rs[:, :], gamma_bc[:, :], rs_sb[:, :], None, ALU.mult).then_inc(rs_step, 1)
            query_lo(None, 3)
            dve.wait_ge(mask_in, 32)
            dve.tensor_scalar(attend[:, :], mask_sb[:, :], 0.5, None, ALU.is_gt).then_inc(mask_step, 1)
            dve.wait_ge(mask_step, 1)
            dve.tensor_scalar(exp_max[:, :], attend[:, :], EXP_HI - EXP_LO, EXP_LO, ALU.mult, ALU.add
                              ).then_inc(mask_step, 1)
            dve.wait_ge(zeroed, 5)
            dve.tensor_copy(bo_hl[0:1, :], bo_raw[0:1, :]).then_inc(bo_step, 1)
            dve.tensor_copy(bo_hi32[32:33, :], bo_raw[32:33, :]).then_inc(bo_step, 1)
            dve.tensor_copy(ones_k[:, :], ones_f[:, :]).then_inc(ones_ok, 1)
            for m in range(KC):
                key_lo(m)
            dve.wait_ge(bo_step, 2)
            dve.tensor_tensor(bo_hl[32:33, :], bo_raw[32:33, :], bo_hi32[32:33, :].bitcast(F32), ALU.subtract
                              ).then_inc(bo_step, 1)
            dve.wait_ge(vones_ok, 2)
            for j in range(2):
                value_blocks(j)
            dve.wait_ge(mask_step, 2)
            dve.wait_ge(rs_step, 5)
            dve.wait_ge(xr_in, 16)
            with dve.Fori(0, B - 1, 1) as b:
                step(b)
            step(B - 1, last=True)

        @block.gpsimd
        def _(pool):
            def ln_power(bb):
                pool.wait_ge(ln_ve_ok, 2 * bb + 2)
                pool.tensor_tensor(ln_rstd[:, :], ln_ve[:, :], minus_half[:, :], ALU.pow).then_inc(ln_rstd_ok, 1)
                pool.wait_ge(ln_rstd_ok, 2 * bb + 1)
                pool.tensor_tensor(ln_bias[:, :], ln_nm[:, :], ln_rstd[:, :], ALU.mult).then_inc(ln_rstd_ok, 1)

            def key_blocks(bb):
                cols = bass.ts(bb, T)
                pool.wait_ge(ln_rstd_ok, 2 * bb + 2)
                for h in range(4):
                    r = slice(HD * h, HD * (h + 1))
                    pool.tensor_copy(kbd[r, :, T * (h % 2):T * (h % 2) + T],
                                     k_hl[r, :, :, cols].rearrange("p a c n -> p (a c) n")).then_inc(kbd_ok, 1)
                pool.wait_ge(kbd_ok, 4 * (bb + 1))

            def add_beta(bb):
                for t in range(NT):
                    xt = xs[:, NT * bb + t, :]
                    pool.tensor_tensor(xt, xt, beta_bc[:, :], ALU.add).then_inc(xb_ok, 1)

            def power(dst, src, ready, done, n):
                pool.wait_ge(ready, n)
                pool.tensor_tensor(dst, src, minus_half[:, 0:1], ALU.pow).then_inc(done, 1)

            def residual_powers(b, t):
                power(d_rstd[:, t:t + 1], d_ve[:, t:t + 1], d_ve_ok, d_rstd_ok, NT * b + t + 1)
                power(n_rstd[:, t:t + 1], n_ve[:, t:t + 1], n_ve_ok, n_rstd_ok, NT * b + t + 1)

            def rivals(b, j):
                n, ts = 2 * b + j + 1, slice(2 * j, 2 * j + 2)
                mine = lg[:, ts, :].unsqueeze(3).broadcast_to([P, 2, E, E])
                other = lg[:, ts, :].unsqueeze(2).broadcast_to([P, 2, E, E])
                pool.wait_ge(lg_ok, n)
                pool.tensor_tensor(diff[:, ts, :, :], other, mine, ALU.subtract).then_inc(diff_ok, 1)

            def step(b, last=False):
                if not last:
                    ln_power(b + 1)
                    pool.wait_ge(s_full, NP * b + NP)
                    key_blocks(b + 1)
                for t in range(NT):
                    residual_powers(b, t)
                rivals(b, 0)
                rivals(b, 1)
                if not last:
                    pool.wait_ge(hs_ok, NT * (b + 2))
                    add_beta(b + 1)

            pool.memset(minus_half[:, :], -0.5).then_inc(half_ok, 1)
            pool.memset(ident[:, :], 0.0).then_inc(zeroed, 1)
            pool.memset(least[:, :, :], -FLT_MIN).then_inc(zeroed, 1)
            pool.memset(ctx_clean[:, :, :], 0.0).then_inc(zeroed, 1)
            pool.wait_ge(zeroed, 3)
            pool.affine_select(out=ident[:, :], in_=ident[:, :], compare_op=ALU.not_equal, fill=1.0, base=0,
                               pattern=[[-1, P]], channel_multiplier=1).then_inc(ident_ok, 1)
            pool.wait_ge(half_ok, 1)
            ln_power(0)
            pool.affine_select(out=least[:, :, :], in_=least[:, :, :], compare_op=ALU.is_gt, fill=0.0, base=0,
                               pattern=[[1, E], [-1, E]], channel_multiplier=0).then_inc(least_ok, 1)
            pool.memset(ones_f[:, :], 1.0).then_inc(zeroed, 1)
            pool.memset(bo_hl[:, :].bitcast(F32), 0.0).then_inc(zeroed, 1)
            pool.memset(kbd[:, :, :].bitcast(F32), 0.0).then_inc(zeroed, 1)
            pool.memset(vbd[:, :, :, :], 0.0).then_inc(zeroed, 1)
            pool.wait_ge(zeroed, 7)
            for s in range(2):
                pool.memset(vbd[s * T:(s + 1) * T, :, :, 2 * HD + s], ONE).then_inc(vones_ok, 1)
            pool.wait_ge(vones_ok, 2)
            pool.wait_ge(small_in, SMALL)
            pool.wait_ge(hs_ok, NT)
            add_beta(0)
            pool.wait_ge(wo_in, 16)
            for c in range(KC):
                pool.wait_ge(wo_hi_ok, c + 1)
                pool.tensor_tensor(wo_lo[:, c, :], wo_raw[:, c, :], wo_hi[:, c, :].bitcast(F32), ALU.subtract
                                   ).then_inc(wo_lo_ok, 1)
            pool.wait_ge(ffn_in, 48)
            pool.wait_ge(ffn_hi_ok, 2)
            pool.tensor_tensor(dr_lo[:, :, :], dr_raw[:, :, :], dr_hi[:, :, :].bitcast(F32), ALU.subtract
                               ).then_inc(ffn_lo_ok, 1)
            pool.tensor_tensor(up_lo[:, :], up_raw[:, :], up_hi[:, :].bitcast(F32), ALU.subtract
                               ).then_inc(ffn_lo_ok, 1)
            pool.wait_ge(ffn_lo_ok, 2)
            pool.wait_ge(mm_free, mm(None, "K3")[0] + 1)
            key_blocks(0)
            pool.wait_ge(least_ok, 1)
            with pool.Fori(0, B - 1, 1) as b:
                step(b)
            step(B - 1, last=True)


def _transposed(a):
    return np.ascontiguousarray(np.swapaxes(a, -1, -2))


def kernel(x, ctx_2048, mask_BxS2_ik0, L0_xattn_Wq, L0_xattn_bq, L0_xattn_Wk, L0_xattn_bk, L0_xattn_Wv, L0_xattn_bv,
           L0_xattn_Wo, L0_xattn_bo, L0_xattn_ln_gamma, L0_xattn_ln_beta, L0_xattn_residual_scale, L0_ffn_router_w,
           L0_ffn_down_w, L0_ffn_up_w):
    import concourse.bacc as bacc
    from concourse.bass_utils import run_bass_kernel_spmd

    a = lambda v: np.ascontiguousarray(np.asarray(v))
    H = x.shape[-1]
    arrays = {
        "x": a(x),
        "ctx_t": _transposed(a(ctx_2048).reshape(-1, H)),
        "mask_t": _transposed(a(mask_BxS2_ik0)),
        "wq_t": _transposed(a(L0_xattn_Wq)),
        "bq": _transposed(a(L0_xattn_bq).reshape(-1, P)),
        "wk_t": _transposed(a(L0_xattn_Wk)),
        "bk": _transposed(a(L0_xattn_bk).reshape(-1, P)),
        "wv_t": _transposed(a(L0_xattn_Wv)),
        "bv": a(L0_xattn_bv),
        "wo_t": _transposed(a(L0_xattn_Wo)),
        "bo": a(L0_xattn_bo),
        "gamma": a(L0_xattn_ln_gamma),
        "beta": a(L0_xattn_ln_beta),
        "rs": a(L0_xattn_residual_scale).reshape(1, 1),
        "router_t": _transposed(a(L0_ffn_router_w)),
        "down_t": _transposed(a(L0_ffn_down_w).reshape(-1, H)),
        "up_t": a(_transposed(a(L0_ffn_up_w))).reshape(-1, H),
    }
    nc = bacc.Bacc("TRN2", target_bir_lowering=False, num_devices=1)
    args = [nc.dram_tensor(n, v.shape, mybir.dt.from_np(v.dtype), kind="ExternalInput").ap() for n, v in arrays.items()]
    args.append(nc.dram_tensor("out", x.shape, mybir.dt.float32, kind="ExternalOutput").ap())
    build(nc, *args)
    r = run_bass_kernel_spmd(nc, [arrays], core_ids=[0])
    return r.results[0]["out"]
```

```python
from contextlib import ExitStack

import numpy as np

import concourse.bass as bass
from concourse import mybir

ALU = mybir.AluOpType
ACT = mybir.ActivationFunctionType
AX = mybir.AxisListType
F32 = mybir.dt.float32
F32R = mybir.dt.float32r
I32 = mybir.dt.int32
U8 = mybir.dt.uint8

P = 128
NH = 16
E = 8
EPS = 1e-5
RES_SCALE_MAX = 0.3
CLIP = 50.0
LIM = 10000.0
FLT_MAX = float(np.finfo(np.float32).max)
FLT_MIN = float(np.finfo(np.float32).tiny)

R_STEP = ["S0", "S1", "S2", "S3", "S4", "S5", "S6", "S7", "Q0", "W0", "W1", "Q1", "U0", "U1", "U2", "U3", "W2", "W3",
          "Q2", "Q3"]
T_STEP = ["n0", "n1", "h0", "h1", "h2", "h3", "n2", "n3", "c0", "c1", "a0", "c2", "c3", "a1"]
V_STEP = ["f0", "v00", "v01", "v10", "v11", "v20", "v21", "f1", "v30", "v31"]
R_BEFORE = ["Q0", "Q1", "Q2", "Q3", "K0", "K1", "K2", "K3", "V0", "V1"]
T_BEFORE = ["h0", "h1", "h2", "h3"]
NEXT, PREVIOUS = "Qh", "nfaU"
BEFORE, AFTER = -1, 4


class Ring:

    def __init__(self, banks, order, before=()):
        self.banks = banks
        steps = range(AFTER)
        self.parts = {BEFORE: list(before)}
        for b in steps:
            self.parts[b] = [u for u in order if not (b == steps[0] and u[0] in PREVIOUS)
                             and not (b == steps[-1] and u[0] in NEXT)]
        self.parts[AFTER] = [u for u in order if u[0] in PREVIOUS]
        self.all = [(part, u) for part, uses in self.parts.items() for u in uses]

    def bank(self, part, use):
        if isinstance(part, int):
            return self.all.index((part, use)) % self.banks
        first, second = self.bank(1, use), self.bank(2, use)
        assert first == second
        return first

    def count(self, part, use):
        if isinstance(part, int):
            scores = use[0] == "S"
            return sum((u[0] == "S") == scores for _, u in self.all[:self.all.index((part, use)) + 1])
        first, second = self.count(1, use), self.count(2, use)
        return (part - 1) * (second - first) + first

    def freed(self, part, use):
        if isinstance(part, int):
            at = self.all.index((part, use)) - self.banks
            return None if at < 0 else (self.all[at][1][0] == "S", self.count(*self.all[at]))
        (kind, first), (same_kind, second) = self.freed(1, use), self.freed(2, use)
        assert kind == same_kind
        return kind, (part - 1) * (second - first) + first


def build(nc, x, ctx_t, mask_t, wq_t, bq, wk_t, bk, wv_t, bv, wo_t, bo, gamma, beta, rs, router_t, down_t, up_t, out):
    B, S, H = x.shape
    T = ctx_t.shape[1] // B
    HD = H // NH
    EI = up_t.shape[0]
    EXP_I = EI // E
    KC = H // P
    NT = S // P
    NP = NH // 2
    VW = 2 * HD + 2
    FW = EI + E
    SCALE = 1.0 / float(np.sqrt(HD))
    EXP_HI = float(np.exp(np.float64(CLIP)))
    EXP_LO = float(np.exp(np.float64(-CLIP)))
    ONE = 1.0 + 1e-8
    assert T * 2 == P and H % P == 0 and S == NT * P and HD == 32 and NT == 4 and EI == P

    ring_r = Ring(4, R_STEP, R_BEFORE)
    ring_t = Ring(2, T_STEP, T_BEFORE)
    ring_v = Ring(2, V_STEP)
    assert B == AFTER

    stack = ExitStack()
    with stack:
        def sb(name, shape, dt=F32):
            return stack.enter_context(nc.sbuf_tensor(name, shape, dt))

        def sem(name):
            return stack.enter_context(nc.semaphore(name))

        def split(name, shape):
            return sb(name + "_hi", shape, F32R), sb(name + "_lo", shape, F32R)

        xs = sb("xs", [P, B * NT, H])
        stage = sb("stage", [P, 2 * KC, H])
        wq_raw, wo_raw, probs = stage[:, 0:KC, :], stage[:, KC:, :], stage[:, :, :]
        wk = sb("wk", [P, KC, H])
        att, x1n = wk, wk
        wv = sb("wv", [P, KC, H])
        hs, cen = wv, wv
        ctx_sb = wo_raw[:, 0:2, :].rearrange("p a n -> p (a n)").rearrange("p (k n) -> p k n", k=KC)
        wq_hi, wq_lo = split("wq", [P, KC, H])
        wo_hi, wo_lo = split("wo", [P, KC, H])
        dr_raw = sb("dr_raw", [P, KC, FW])
        dr_flat = dr_raw[:, :, :].rearrange("p k n -> p (k n)")
        vbd = dr_flat[:, 0:NP * VW].rearrange("p (n w) -> p n w", n=NP)
        ctx_words = KC * B * T // 4
        ctx_notnan, ctx_finite = (
            dr_flat[:, i * ctx_words:(i + 1) * ctx_words].bitcast(U8).rearrange("p (k n) -> p k n", k=KC)
            for i in range(2))
        dr_hi, dr_lo = split("dr", [P, KC, FW])
        up_raw = sb("up_raw", [EI, H])
        up_hi, up_lo = split("up", [EI, H])
        compare = sb("compare", [P, 4, NT * E * E])
        ctx_clean = compare[:, :, :]
        k_hl = sb("k_hl", [P, 2, KC, B * T], F32R)
        kbd = sb("kbd", [P, 2 * KC, 2, 2 * T], F32R)
        vbd_all = sb("vbd_all", [P, B, NP, VW])
        q_hi, q_lo = split("q", [P, KC, S])
        hst_hi, hst_lo = split("hst", [P, NT, KC, P])
        attt_hi, attt_lo = split("attt", [P, NT, KC, P])
        x1t_hi, x1t_lo = attt_hi, attt_lo
        hidden = sb("hidden", [P, 3 * NT, EI])
        hid_tanh, hid, hidg = (hidden[:, i * NT:(i + 1) * NT, :] for i in range(3))
        hid_out = hidden[:, 2 * NT:, :].rearrange("p t n -> p (t n)")
        ctx_lim = hidden[:, 0:2 * NT, :].rearrange("p t n -> p (t n)").rearrange("p (k n) -> p k n", k=KC)
        hidt_hi, hidt_lo = split("hidt", [EI, NT, P])

        ident = sb("ident", [P, P])
        least = sb("least", [P, E, E])
        ones_k = sb("ones_k", [33, P], F32R)
        ones_f = sb("ones_f", [33, P])
        bo_raw = hid_out[0:33, :]
        bo_hl = sb("bo_hl", [33, H], F32R)
        bo_hi32 = hidt_hi[0:33, :, :].rearrange("p t n -> p (t n)")
        gamma_bc = sb("gamma_bc", [P, H])
        gamma_rs = gamma_bc
        beta_bc = sb("beta_bc", [P, H])
        bv_bc = sb("bv_bc", [P, H])
        bq_sb = sb("bq_sb", [P, KC])
        bk_sb = sb("bk_sb", [P, KC])
        rs_raw = sb("rs_raw", [P, 1])
        rs_sb = sb("rs_sb", [P, 1])
        rs_sq = sb("rs_sq", [P, 1])
        mask_sb = sb("mask_sb", [P, B], I32)
        attend = sb("attend", [P, B])
        exp_max = sb("exp_max", [P, B])
        exp_min = sb("exp_min", [P, 1])
        eps_sb = sb("eps_sb", [P, 1])
        minus_half = sb("minus_half", [P, B * NT])

        ln_st = sb("ln_st", [P, B * NT, 6])
        ln_mv = sb("ln_mv", [P, B * NT, 2])
        ln_ve = sb("ln_ve", [P, B * NT])
        ln_nm = sb("ln_nm", [P, B * NT])
        ln_rstd = sb("ln_rstd", [P, B * NT])
        ln_bias = sb("ln_bias", [P, B * NT])
        d_st = sb("d_st", [P, NT, 6])
        d_mv = sb("d_mv", [P, NT, 2])
        d_ve = sb("d_ve", [P, NT])
        d_rstd = sb("d_rstd", [P, NT])
        n_st = sb("n_st", [P, NT, 6])
        n_mv = sb("n_mv", [P, NT, 2])
        n_ve = sb("n_ve", [P, NT])
        n_rstd = sb("n_rstd", [P, NT])
        n_nm = sb("n_nm", [P, NT])
        n_bias = sb("n_bias", [P, NT])
        rz = sb("rz", [P, NT, 2, 4, 2])
        lg = sb("lg", [P, NT, E])
        lmax = sb("lmax", [P, NT])
        lsub = sb("lsub", [P, NT, E])
        lexp = sb("lexp", [P, NT, E])
        diff, beats = (compare[:, i, :].rearrange("p (t e f) -> p t e f", t=NT, e=E) for i in range(2))
        rank = sb("rank", [P, NT, E])
        kept = sb("kept", [P, NT, E])
        lsum = sb("lsum", [P, NT])
        lrec = sb("lrec", [P, NT])
        gate = sb("gate", [P, NT, E])

        def banks(name, n):
            return [stack.enter_context(nc.psum_tensor(f"{name}{i}", [P, 512], F32)) for i in range(n)]

        ps_r, ps_t, ps_v = banks("ps_r", 4), banks("ps_t", 2), banks("ps_v", 2)

        x0_in, xr_in, ctx_in, wq_in, wk_in, wv_in, wo_in, ffn_in, small_in, mask_in = [
            sem(n) for n in ("x0_in", "xr_in", "ctx_in", "wq_in", "wk_in", "wv_in", "wo_in", "ffn_in", "small_in",
                             "mask_in")]
        stored = sem("stored")
        mm_full, mm_free, t_full, t_free = sem("mm_full"), sem("mm_free"), sem("t_full"), sem("t_free")
        s_full, v_full, v_free = sem("s_full"), sem("v_full"), sem("v_free")
        zeroed, ident_ok, half_ok, least_ok, ones_ok = (
            sem("zeroed"), sem("ident_ok"), sem("half_ok"), sem("least_ok"), sem("ones_ok"))
        bo_step, rs_step, mask_step, vones_ok, gamma_ok = (
            sem("bo_step"), sem("rs_step"), sem("mask_step"), sem("vones_ok"), sem("gamma_ok"))
        ctx_part, ctx_ok = sem("ctx_part"), sem("ctx_ok")
        wq_hi_ok, wq_lo_ok, wo_hi_ok, wo_lo_ok, ffn_hi_ok, ffn_lo_ok = [
            sem(n) for n in ("wq_hi_ok", "wq_lo_ok", "wo_hi_ok", "wo_lo_ok", "ffn_hi_ok", "ffn_lo_ok")]
        k_hi_ok, v_ok, kbd_ok, vbd_ok = sem("k_hi_ok"), sem("v_ok"), sem("kbd_ok"), sem("vbd_ok")
        ln_st_ok, ln_mv_ok, ln_ve_ok, ln_rstd_ok, hs_ok = (
            sem("ln_st_ok"), sem("ln_mv_ok"), sem("ln_ve_ok"), sem("ln_rstd_ok"), sem("hs_ok"))
        hst_hi_ok, q_hi_ok = sem("hst_hi_ok"), sem("q_hi_ok")
        exp_ok, probs_ok = sem("exp_ok"), sem("probs_ok")
        rz_ok = sem("rz_ok")
        attt_hi_ok = sem("attt_hi_ok")
        xb_ok = sem("xb_ok")
        d_st_ok, d_mv_ok, d_ve_ok, d_rstd_ok, cen_ok, x1_ok = (
            sem("d_st_ok"), sem("d_mv_ok"), sem("d_ve_ok"), sem("d_rstd_ok"), sem("cen_ok"), sem("x1_ok"))
        n_st_ok, n_mv_ok, n_ve_ok, n_rstd_ok, x1n_ok, x1t_hi_ok = (
            sem("n_st_ok"), sem("n_mv_ok"), sem("n_ve_ok"), sem("n_rstd_ok"), sem("x1n_ok"), sem("x1t_hi_ok"))
        tanh_ok, lg_ok, lmax_ok, lsub_ok, lexp_ok = (
            sem("tanh_ok"), sem("lg_ok"), sem("lmax_ok"), sem("lsub_ok"), sem("lexp_ok"))
        diff_ok, beats_ok, rank_ok, kept_ok, lsum_ok, lrec_ok, gate_ok, hid_ok, hidg_ok, hidt_hi_ok = [
            sem(n) for n in ("diff_ok", "beats_ok", "rank_ok", "kept_ok", "lsum_ok", "lrec_ok", "gate_ok",
                             "hid_ok", "hidg_ok", "hidt_hi_ok")]

        block = stack.enter_context(nc.Block())

        def wide(w):
            return w.rearrange("(k p) n -> p k n", p=P)

        x_tiles = x.rearrange("b (t p) h -> p (b t) h", p=P)
        out_tiles = out.rearrange("b (t p) h -> p (b t) h", p=P)
        SMALL = 16 * 8

        @block.sync
        def _(sp):
            for t in range(NT):
                sp.dma_start(xs[:, t, :], x_tiles[:, t, :]).then_inc(x0_in, 16)
            sp.dma_start(wq_raw[:, :, :], wide(wq_t)).then_inc(wq_in, 16)
            sp.dma_start(ctx_sb[:, :, :], wide(ctx_t)).then_inc(ctx_in, 16)
            sp.dma_start(wk[:, :, :], wide(wk_t)).then_inc(wk_in, 16)
            sp.dma_start(xs[:, NT:, :], x_tiles[:, NT:, :]).then_inc(xr_in, 16)
            sp.wait_ge(t_full, NT)
            sp.dma_start(wv[:, :, :], wide(wv_t)).then_inc(wv_in, 16)
            sp.wait_ge(ctx_ok, 1)
            sp.dma_start(wo_raw[:, :, :], wide(wo_t)).then_inc(wo_in, 16)
            sp.dma_start(dr_raw[:, :, 0:EI], wide(down_t)).then_inc(ffn_in, 16)
            sp.dma_start(dr_raw[:, :, EI:FW], wide(router_t)).then_inc(ffn_in, 16)
            sp.dma_start(up_raw[:, :], up_t).then_inc(ffn_in, 16)

            def store(part, bb):
                for t in range(NT):
                    sp.wait_ge(mm_free, ring_r.count(part, f"U{t}"))
                    sp.dma_start(out_tiles[:, bass.ds(NT * bb + t, 1), :],
                                 xs[:, bass.ds(NT * bb + t, 1), :]).then_inc(stored, 16)

            with sp.Fori(1, B - 1, 1) as b:
                store(b, b - 1)
            store(B - 1, B - 2)
            store(AFTER, B - 1)
            sp.wait_ge(stored, 16 * B * NT)

        def rows(v, n):
            return v.rearrange("(a h) -> a h", a=1).broadcast_to([n, H])

        @block.tensor
        def _(pe):
            def passes(dst, pairs, start=True, stop=True):
                n = len(pairs)
                for i, (w, m) in enumerate(pairs):
                    last = pe.matmul(dst, w, m, start=start and i == 0, stop=stop and i == n - 1)
                return last

            def three(hi_w, lo_w, hi_m, lo_m):
                return [(hi_w, hi_m), (hi_w, lo_m), (lo_w, hi_m)]

            def take(ring, part, use, free=mm_free):
                freed = ring.freed(part, use)
                if freed:
                    pe.wait_ge(exp_ok if freed[0] else free, freed[1])
                return ring.bank(part, use)

            def transposes(part, use, src):
                bank = ps_t[take(ring_t, part, use, t_free)]
                for c in range(len(src)):
                    mmi = pe.transpose(bank[:, c * P:(c + 1) * P], src[c], ident[:, :])
                mmi.then_inc(t_full, 1)

            def chunks(buffer, t):
                return [buffer[:, t, c * P:(c + 1) * P] for c in range(KC)]

            def hs_transpose(part, bb, t):
                pe.wait_ge(hs_ok, NT * bb + t + 1)
                transposes(part, f"h{t}", chunks(hs, t))

            def query(part, m):
                k = take(ring_r, part, f"Q{m}")
                if m == 0:
                    pe.wait_ge(t_free, ring_t.count(part, "h3"))
                pairs = []
                for c in range(KC):
                    cols = slice(m * P, (m + 1) * P)
                    pairs += three(wq_hi[:, c, cols], wq_lo[:, c, cols], hst_hi[:, :, c, :], hst_lo[:, :, c, :])
                passes(ps_r[k][:, :], pairs).then_inc(mm_full, 1)

            def keys(m):
                k = take(ring_r, BEFORE, f"K{m}")
                passes(ps_r[k][:, 0:B * T], [(wk[:, c, m * P:(m + 1) * P], ctx_clean[:, c, :]) for c in range(KC)]
                       ).then_inc(mm_full, 1)

            def values(j):
                k = take(ring_r, BEFORE, f"V{j}")
                passes(ps_r[k][:, :], [(ctx_clean[:, c, j * P:(j + 1) * P], wv[:, c, :]) for c in range(KC)]
                       ).then_inc(mm_full, 1)

            def scores(b, p):
                k = take(ring_r, b, f"S{p}")
                c, i = p // 2, p % 2
                passes(ps_r[k][:, :],
                       three(kbd[:, c, i, :], kbd[:, KC + c, i, :], q_hi[:, c, :], q_lo[:, c, :])).then_inc(s_full, 1)

            def weigh(b, t, g):
                k = take(ring_v, b, f"v{t}{g}", v_free)
                if t == 0:
                    pe.wait_ge(probs_ok, NP * b + 4 * g + 4)
                for i in range(4):
                    p = 4 * g + i
                    mmi = pe.matmul(ps_v[k][:, i * VW:(i + 1) * VW], probs[:, p, t * P:(t + 1) * P],
                                    vbd[:, p, :], start=True, stop=True)
                mmi.then_inc(v_full, 1)

            def att_transpose(b, t):
                pe.wait_ge(v_free, ring_v.count(b, f"v{t}1"))
                transposes(b, f"c{t}", chunks(att, t))

            def project(b, t):
                pe.wait_ge(t_free, ring_t.count(b, f"c{t}"))
                k = take(ring_r, b, f"W{t}")
                pairs = [(ones_k[:, :], bo_hl[:, :])]
                for c in range(KC):
                    pairs += three(attt_hi[:, t, c, :], attt_lo[:, t, c, :], wo_hi[:, c, :], wo_lo[:, c, :])
                passes(ps_r[k][:, :], pairs).then_inc(mm_full, 1)

            def x1n_transpose(part, bb, t):
                pe.wait_ge(x1n_ok, NT * bb + t + 1)
                transposes(part, f"n{t}", chunks(x1n, t))

            def down(part, j):
                k = take(ring_v, part, f"f{j}", v_free)
                for i in range(2):
                    t = 2 * j + i
                    pe.wait_ge(t_free, ring_t.count(part, f"n{t}"))
                    pairs = []
                    for c in range(KC):
                        pairs += three(x1t_hi[:, t, c, :], x1t_lo[:, t, c, :], dr_hi[:, c, :], dr_lo[:, c, :])
                    mmi = passes(ps_v[k][:, i * FW:(i + 1) * FW], pairs)
                mmi.then_inc(v_full, 1)

            def hid_transpose(part, bb, j):
                pe.wait_ge(hidg_ok, 2 * bb + j + 1)
                transposes(part, f"a{j}", [hidg[:, 2 * j + i, :] for i in range(2)])

            def up(part, t):
                if t % 2 == 0:
                    pe.wait_ge(t_free, ring_t.count(part, f"a{t // 2}"))
                k = take(ring_r, part, f"U{t}")
                passes(ps_r[k][:, :], three(hidt_hi[:, t, :], hidt_lo[:, t, :], up_hi[:, :], up_lo[:, :])
                       ).then_inc(mm_full, 1)

            def step(b, experts=True, ahead=True):
                pe.wait_ge(kbd_ok, 4 * (b + 1))
                for p in range(4):
                    scores(b, p)
                if experts:
                    x1n_transpose(b, b - 1, 0)
                    x1n_transpose(b, b - 1, 1)
                if ahead:
                    hs_transpose(b, b + 1, 0)
                    hs_transpose(b, b + 1, 1)
                scores(b, 4)
                scores(b, 5)
                if experts:
                    down(b, 0)
                scores(b, 6)
                scores(b, 7)
                if ahead:
                    hs_transpose(b, b + 1, 2)
                    hs_transpose(b, b + 1, 3)
                if experts:
                    x1n_transpose(b, b - 1, 2)
                    x1n_transpose(b, b - 1, 3)
                pe.wait_ge(vbd_ok, b + 1)
                weigh(b, 0, 0)
                weigh(b, 0, 1)
                weigh(b, 1, 0)
                weigh(b, 1, 1)
                if ahead:
                    query(b, 0)
                att_transpose(b, 0)
                att_transpose(b, 1)
                weigh(b, 2, 0)
                weigh(b, 2, 1)
                project(b, 0)
                if experts:
                    down(b, 1)
                    hid_transpose(b, b - 1, 0)
                weigh(b, 3, 0)
                weigh(b, 3, 1)
                project(b, 1)
                att_transpose(b, 2)
                att_transpose(b, 3)
                if ahead:
                    query(b, 1)
                if experts:
                    hid_transpose(b, b - 1, 1)
                    for t in range(NT):
                        up(b, t)
                project(b, 2)
                project(b, 3)
                if ahead:
                    query(b, 2)
                    query(b, 3)

            pe.wait_ge(ident_ok, 1)
            for t in range(NT):
                hs_transpose(BEFORE, 0, t)
            pe.wait_ge(wq_hi_ok, KC)
            pe.wait_ge(wq_lo_ok, KC)
            for m in range(KC):
                query(BEFORE, m)
            pe.wait_ge(ctx_ok, 1)
            pe.wait_ge(wk_in, 16)
            for m in range(KC):
                keys(m)
            pe.wait_ge(wv_in, 16)
            for j in range(2):
                values(j)
            pe.wait_ge(wo_hi_ok, KC)
            pe.wait_ge(wo_lo_ok, KC)
            pe.wait_ge(bo_step, 3)
            pe.wait_ge(ones_ok, 1)
            step(0, experts=False)
            pe.wait_ge(ffn_hi_ok, 2)
            pe.wait_ge(ffn_lo_ok, 2)
            with pe.Fori(1, B - 1, 1) as b:
                step(b)
            step(B - 1, ahead=False)
            x1n_transpose(AFTER, B - 1, 0)
            x1n_transpose(AFTER, B - 1, 1)
            down(AFTER, 0)
            x1n_transpose(AFTER, B - 1, 2)
            x1n_transpose(AFTER, B - 1, 3)
            down(AFTER, 1)
            hid_transpose(AFTER, B - 1, 0)
            up(AFTER, 0)
            up(AFTER, 1)
            hid_transpose(AFTER, B - 1, 1)
            up(AFTER, 2)
            up(AFTER, 3)

        @block.scalar
        def _(act):
            def hi(part, use, dst, done):
                act.wait_ge(t_full, ring_t.count(part, use))
                c = dst.shape[1]
                act.copy(dst, ps_t[ring_t.bank(part, use)][:, 0:c * P].rearrange("p (c n) -> p c n", c=c)
                         ).then_inc(done, 1)

            def hs_norm(bb, t):
                act.wait_ge(ln_rstd_ok, 2 if isinstance(bb, int) and bb == 0 else 4)
                if not (isinstance(bb, int) and bb < 2):
                    act.wait_ge(x1_ok, NT * (bb - 2) + t + 1)
                tile = NT * bb + t
                act.activation(hs[:, t, :], xs[:, bass.ds(tile, 1), :], ACT.Identity,
                               bias=ln_bias[:, bass.ds(tile, 1)], scale=ln_rstd[:, bass.ds(tile, 1)]
                               ).then_inc(hs_ok, 1)

            def x1_norm(bb, t):
                act.wait_ge(n_rstd_ok, 2 * (NT * bb + t + 1))
                act.activation(x1n[:, t, :], xs[:, NT * bb + t, :], ACT.Identity, bias=n_bias[:, t:t + 1],
                               scale=n_rstd[:, t:t + 1]).then_inc(x1n_ok, 1)

            def query_hi(part, m):
                act.wait_ge(mm_full, ring_r.count(part, f"Q{m}"))
                act.activation(q_hi[:, m, :], ps_r[ring_r.bank(part, f"Q{m}")][:, :], ACT.Identity,
                               bias=bq_sb[:, m:m + 1]).then_inc(q_hi_ok, 1)

            def key_hi(m):
                act.wait_ge(mm_full, ring_r.count(BEFORE, f"K{m}"))
                act.activation(k_hl[:, 0, m, :], ps_r[ring_r.bank(BEFORE, f"K{m}")][:, 0:B * T], ACT.Identity,
                               bias=bk_sb[:, m:m + 1]).then_inc(k_hi_ok, 1)

            def exp_scores(b, p):
                act.wait_ge(s_full, NP * b + p + 1)
                act.activation(probs[:, p, :], ps_r[ring_r.bank(b, f"S{p}")][:, :], ACT.Exp, scale=SCALE
                               ).then_inc(exp_ok, 1)

            def hs_hi(part, t):
                hi(part, f"h{t}", hst_hi[:, t, :, :], hst_hi_ok)

            def att_hi(b, t):
                hi(b, f"c{t}", attt_hi[:, t, :, :], attt_hi_ok)

            def x1_hi(part, t):
                hi(part, f"n{t}", x1t_hi[:, t, :, :], x1t_hi_ok)

            def hid_hi(part, j):
                hi(part, f"a{j}", hidt_hi[:, 2 * j:2 * j + 2, :], hidt_hi_ok)

            def hidden_tanh(part, j):
                act.wait_ge(v_full, ring_v.count(part, f"f{j}"))
                f = ps_v[ring_v.bank(part, f"f{j}")][:, 0:2 * FW].rearrange("p (i f) -> p i f", i=2)
                act.activation(hid_tanh[:, 2 * j:2 * j + 2, :], f[:, :, 0:EI], ACT.Tanh, scale=0.5
                               ).then_inc(tanh_ok, 1)

            def exp_logits(bb, j):
                act.wait_ge(lsub_ok, 2 * bb + j + 1)
                act.activation(lexp[:, 2 * j:2 * j + 2, :], lsub[:, 2 * j:2 * j + 2, :], ACT.Exp).then_inc(lexp_ok, 1)

            def step(b, experts=True, ahead=True):
                for p in range(4):
                    exp_scores(b, p)
                if ahead:
                    hs_norm(b + 1, 0)
                    hs_norm(b + 1, 1)
                if experts:
                    x1_hi(b, 0)
                    x1_hi(b, 1)
                if ahead:
                    hs_hi(b, 0)
                    hs_hi(b, 1)
                exp_scores(b, 4)
                exp_scores(b, 5)
                if ahead:
                    hs_norm(b + 1, 2)
                    hs_norm(b + 1, 3)
                if experts:
                    x1_norm(b - 1, 2)
                    x1_norm(b - 1, 3)
                    hidden_tanh(b, 0)
                exp_scores(b, 6)
                exp_scores(b, 7)
                if ahead:
                    hs_hi(b, 2)
                    hs_hi(b, 3)
                if experts:
                    exp_logits(b - 1, 0)
                    x1_hi(b, 2)
                    x1_hi(b, 3)
                if ahead:
                    query_hi(b, 0)
                att_hi(b, 0)
                att_hi(b, 1)
                if experts:
                    hidden_tanh(b, 1)
                    exp_logits(b - 1, 1)
                    hid_hi(b, 0)
                att_hi(b, 2)
                att_hi(b, 3)
                if ahead:
                    query_hi(b, 1)
                if experts:
                    hid_hi(b, 1)
                x1_norm(b, 0)
                x1_norm(b, 1)
                if ahead:
                    query_hi(b, 2)
                    query_hi(b, 3)

            act.dma_start(bq_sb[:, :], bq).then_inc(small_in, 16)
            act.dma_start(bk_sb[:, :], bk).then_inc(small_in, 16)
            act.dma_start(rs_raw[:, :], rs.broadcast_to([P, 1])).then_inc(small_in, 16)
            act.dma_start(bo_raw[0:1, :], rows(bo, 1)).then_inc(small_in, 16)
            act.dma_start(bo_raw[32:33, :], rows(bo, 1)).then_inc(small_in, 16)
            for half in range(2):
                act.dma_start(mask_sb[half * T:(half + 1) * T, :], mask_t).then_inc(mask_in, 16)
            act.dma_start(gamma_bc[:, :], rows(gamma, P)).then_inc(small_in, 16)
            act.dma_start(beta_bc[:, :], rows(beta, P)).then_inc(small_in, 16)
            act.dma_start(bv_bc[:, :], rows(bv, P)).then_inc(small_in, 16)
            for t in range(NT):
                hs_norm(0, t)
            act.wait_ge(wq_in, 16)
            for c in range(KC):
                act.copy(wq_hi[:, c, :], wq_raw[:, c, :]).then_inc(wq_hi_ok, 1)
            for t in range(NT):
                hs_hi(BEFORE, t)
            act.wait_ge(small_in, SMALL)
            for m in range(KC):
                query_hi(BEFORE, m)
            for m in range(KC):
                key_hi(m)
            act.wait_ge(wo_in, 16)
            for c in range(KC):
                act.copy(wo_hi[:, c, :], wo_raw[:, c, :]).then_inc(wo_hi_ok, 1)
            act.wait_ge(ffn_in, 48)
            act.copy(dr_hi[:, :, :], dr_raw[:, :, :]).then_inc(ffn_hi_ok, 1)
            act.copy(up_hi[:, :], up_raw[:, :]).then_inc(ffn_hi_ok, 1)
            act.wait_ge(wq_lo_ok, KC)
            act.wait_ge(wo_lo_ok, KC)
            step(0, experts=False)
            with act.Fori(1, B - 1, 1) as b:
                step(b)
            step(B - 1, ahead=False)
            x1_hi(AFTER, 0)
            x1_hi(AFTER, 1)
            x1_norm(B - 1, 2)
            x1_norm(B - 1, 3)
            hidden_tanh(AFTER, 0)
            exp_logits(B - 1, 0)
            x1_hi(AFTER, 2)
            x1_hi(AFTER, 3)
            hidden_tanh(AFTER, 1)
            exp_logits(B - 1, 1)
            hid_hi(AFTER, 0)
            hid_hi(AFTER, 1)

        @block.vector
        def _(dve):
            def hold(semaphore, value):
                dve.wait_ge(semaphore, value)
                dve.nop(nofuse=True)

            def ln_stats(tiles):
                for t in tiles:
                    dve.bn_stats(ln_st[:, t, :], xs[:, t, :]).then_inc(ln_st_ok, 1)
                for t in tiles:
                    dve.wait_ge(ln_st_ok, t + 1)
                    dve.bn_aggr(ln_mv[:, t, :], ln_st[:, t, :]).then_inc(ln_mv_ok, 1)
                some = slice(tiles[0], tiles[-1] + 1)
                dve.wait_ge(ln_mv_ok, tiles[-1] + 1)
                dve.tensor_scalar(ln_ve[:, some], ln_mv[:, some, 1], EPS, None, ALU.add).then_inc(ln_ve_ok, 1)
                dve.tensor_scalar(ln_nm[:, some], ln_mv[:, some, 0], -1.0, None, ALU.mult).then_inc(ln_ve_ok, 1)

            def lo(part, use, dst, hi_part, hi_ok, n):
                dve.wait_ge(hi_ok, n)
                c = dst.shape[1]
                src = ps_t[ring_t.bank(part, use)][:, 0:c * P].rearrange("p (c n) -> p c n", c=c)
                dve.tensor_tensor(dst, src, hi_part.bitcast(F32), ALU.subtract).then_inc(t_free, 1)

            def hs_lo(part, bb, t):
                lo(part, f"h{t}", hst_lo[:, t, :, :], hst_hi[:, t, :, :], hst_hi_ok, NT * bb + t + 1)

            def att_lo(b, t):
                lo(b, f"c{t}", attt_lo[:, t, :, :], attt_hi[:, t, :, :], attt_hi_ok, NT * b + t + 1)

            def x1_lo(part, bb, t):
                lo(part, f"n{t}", x1t_lo[:, t, :, :], x1t_hi[:, t, :, :], x1t_hi_ok, NT * bb + t + 1)

            def hid_lo(part, bb, j):
                ts = slice(2 * j, 2 * j + 2)
                lo(part, f"a{j}", hidt_lo[:, ts, :], hidt_hi[:, ts, :], hidt_hi_ok, 2 * bb + j + 1)

            def query_lo(part, bb, m):
                dve.wait_ge(q_hi_ok, KC * bb + m + 1)
                dve.scalar_tensor_tensor(q_lo[:, m, :], ps_r[ring_r.bank(part, f"Q{m}")][:, :], bq_sb[:, m:m + 1],
                                         q_hi[:, m, :].bitcast(F32), ALU.add, ALU.subtract).then_inc(mm_free, 1)

            def key_lo(m):
                dve.wait_ge(k_hi_ok, m + 1)
                dve.scalar_tensor_tensor(k_hl[:, 1, m, :], ps_r[ring_r.bank(BEFORE, f"K{m}")][:, 0:B * T],
                                         bk_sb[:, m:m + 1], k_hl[:, 0, m, :].bitcast(F32), ALU.add, ALU.subtract
                                         ).then_inc(mm_free, 1)

            def value_blocks(j):
                bank = ps_r[ring_r.bank(BEFORE, f"V{j}")]
                dve.wait_ge(mm_full, ring_r.count(BEFORE, f"V{j}"))
                for i in range(2):
                    for s in range(2):
                        rows_in, rows_out = slice(i * T, (i + 1) * T), slice(s * T, (s + 1) * T)
                        src = bank[rows_in, :].rearrange("p (n s d) -> p n s d", s=2, d=HD)[:, :, s, :]
                        bias = bv_bc[rows_in, :].rearrange("p (n s d) -> p n s d", s=2, d=HD)[:, :, s, :]
                        final = (i, s) == (1, 1)
                        if final:
                            dve.wait_ge(v_ok, 3 * (j + 1))
                        dve.tensor_tensor(vbd_all[rows_out, 2 * j + i, :, s * HD:(s + 1) * HD], src, bias, ALU.add
                                          ).then_inc(mm_free if final else v_ok, 1)

            def clip(b, p):
                dve.wait_ge(exp_ok, NP * b + p + 1)
                dve.tensor_scalar(probs[:, p, :], probs[:, p, :], exp_min[:, 0:1], exp_max[:, bass.ds(b, 1)],
                                  ALU.max, ALU.min).then_inc(probs_ok, 1)

            def normalise(b, halves):
                def values_of(half):
                    return ps_v[ring_v.bank(b, f"v{half}")][:, 0:4 * VW].rearrange("p (n w) -> p n w", n=4)

                def reciprocals(half):
                    t, g = int(half[0]), int(half[1])
                    dve.wait_ge(v_full, ring_v.count(b, f"v{half}"))
                    dve.reciprocal(rz[:, t, g, :, :], values_of(half)[:, :, 2 * HD:VW]).then_inc(rz_ok, 1)

                def product(half):
                    t, g = int(half[0]), int(half[1])
                    order = [u[1:] for u in V_STEP if u[0] == "v"]
                    dve.wait_ge(rz_ok, 2 * NT * b + order.index(half) + 1)
                    dve.tensor_tensor(att[:, t, 4 * 2 * HD * g:4 * 2 * HD * (g + 1)].rearrange(
                                          "p (n s d) -> p n s d", n=4, s=2),
                                      values_of(half)[:, :, 0:2 * HD].rearrange("p n (s d) -> p n s d", s=2),
                                      rz[:, t, g, :, :].unsqueeze(3).broadcast_to([P, 4, 2, HD]), ALU.mult
                                      ).then_inc(v_free, 1)

                reciprocals(halves[0])
                for half, following in zip(halves, halves[1:]):
                    reciprocals(following)
                    product(half)
                product(halves[-1])

            def centre(b, tiles):
                bank = {t: ps_r[ring_r.bank(b, f"W{t}")] for t in tiles}
                n = {t: NT * b + t + 1 for t in tiles}
                for t in tiles:
                    hold(mm_full, ring_r.count(b, f"W{t}"))
                    dve.bn_stats(d_st[:, t, :], bank[t][:, :]).then_inc(d_st_ok, 1)
                for t in tiles:
                    hold(d_st_ok, n[t])
                    dve.bn_aggr(d_mv[:, t, :], d_st[:, t, :]).then_inc(d_mv_ok, 1)
                for t in tiles:
                    dve.wait_ge(d_mv_ok, n[t])
                    dve.tensor_scalar(d_ve[:, t:t + 1], d_mv[:, t, 1:2], rs_sq[:, :], eps_sb[:, :], ALU.mult, ALU.add
                                      ).then_inc(d_ve_ok, 1)
                for t in tiles:
                    dve.scalar_tensor_tensor(cen[:, t, :], bank[t][:, :], d_mv[:, t, 0:1], gamma_rs[:, :],
                                             ALU.subtract, ALU.mult).then_inc(mm_free, 1)

            def residual(b, tiles):
                n = {t: NT * b + t + 1 for t in tiles}
                x_tile = {t: xs[:, NT * b + t, :] for t in tiles}
                dve.wait_ge(xb_ok, NT * b + NT)
                for t in tiles:
                    dve.wait_ge(mm_free, ring_r.count(b, f"W{t}"))
                    dve.wait_ge(d_rstd_ok, n[t])
                    dve.scalar_tensor_tensor(x_tile[t], cen[:, t, :], d_rstd[:, t:t + 1], x_tile[t], ALU.mult, ALU.add
                                             ).then_inc(x1_ok, 1)
                for t in tiles:
                    hold(x1_ok, n[t])
                    dve.bn_stats(n_st[:, t, :], x_tile[t]).then_inc(n_st_ok, 1)
                for t in tiles:
                    hold(n_st_ok, n[t])
                    dve.bn_aggr(n_mv[:, t, :], n_st[:, t, :]).then_inc(n_mv_ok, 1)
                for t in tiles:
                    dve.wait_ge(n_mv_ok, n[t])
                    dve.tensor_scalar(n_nm[:, t:t + 1], n_mv[:, t, 0:1], -1.0, None, ALU.mult).then_inc(n_ve_ok, 1)
                    dve.tensor_scalar(n_ve[:, t:t + 1], n_mv[:, t, 1:2], EPS, None, ALU.add).then_inc(n_ve_ok, 1)

            def router(part, bb, j):
                n, ts = 2 * bb + j + 1, slice(2 * j, 2 * j + 2)
                f = ps_v[ring_v.bank(part, f"f{j}")][:, 0:2 * FW].rearrange("p (i f) -> p i f", i=2)
                dve.wait_ge(tanh_ok, n)
                dve.tensor_copy(lg[:, ts, :], f[:, :, EI:FW]).then_inc(lg_ok, 1)
                dve.scalar_tensor_tensor(hid[:, ts, :], hid_tanh[:, ts, :], 1.0, f[:, :, 0:EI], ALU.add, ALU.mult
                                         ).then_inc(v_free, 1)
                dve.wait_ge(lg_ok, n)
                dve.tensor_reduce(lmax[:, ts], lg[:, ts, :], AX.X, ALU.max).then_inc(lmax_ok, 1)
                dve.wait_ge(lmax_ok, n)
                dve.tensor_tensor(lsub[:, ts, :], lg[:, ts, :], lmax[:, ts].unsqueeze(2).broadcast_to([P, 2, E]),
                                  ALU.subtract).then_inc(lsub_ok, 1)

            def gating(part, bb, j):
                n, ts = 2 * bb + j + 1, slice(2 * j, 2 * j + 2)
                dve.wait_ge(diff_ok, n)
                dve.tensor_tensor(beats[:, ts, :, :], diff[:, ts, :, :],
                                  least[:, :, :].unsqueeze(1).broadcast_to([P, 2, E, E]), ALU.is_gt
                                  ).then_inc(beats_ok, 1)
                dve.wait_ge(lexp_ok, n)
                dve.tensor_reduce(lsum[:, ts], lexp[:, ts, :], AX.X, ALU.add).then_inc(lsum_ok, 1)
                dve.wait_ge(beats_ok, n)
                dve.tensor_reduce(rank[:, ts, :], beats[:, ts, :, :], AX.X, ALU.add).then_inc(rank_ok, 1)
                dve.wait_ge(lsum_ok, n)
                dve.reciprocal(lrec[:, ts], lsum[:, ts]).then_inc(lrec_ok, 1)
                dve.wait_ge(rank_ok, n)
                dve.scalar_tensor_tensor(kept[:, ts, :], rank[:, ts, :], 1.5, lexp[:, ts, :], ALU.is_lt, ALU.mult
                                         ).then_inc(kept_ok, 1)
                dve.wait_ge(kept_ok, n)
                dve.wait_ge(lrec_ok, n)
                dve.scalar_tensor_tensor(gate[:, ts, :], kept[:, ts, :], 0.5,
                                         lrec[:, ts].unsqueeze(2).broadcast_to([P, 2, E]), ALU.mult, ALU.mult
                                         ).then_inc(gate_ok, 1)
                dve.wait_ge(gate_ok, n)
                dve.wait_ge(v_free, ring_v.count(part, f"f{j}"))
                dve.tensor_tensor(hidg[:, ts, :].rearrange("p t (e i) -> p t e i", e=E),
                                  hid[:, ts, :].rearrange("p t (e i) -> p t e i", e=E),
                                  gate[:, ts, :].unsqueeze(3).broadcast_to([P, 2, E, EXP_I]), ALU.mult
                                  ).then_inc(hidg_ok, 1)

            def finish(part, bb, t):
                dve.wait_ge(mm_full, ring_r.count(part, f"U{t}"))
                xt = xs[:, NT * bb + t, :]
                dve.tensor_tensor(xt, ps_r[ring_r.bank(part, f"U{t}")][:, :], xt, ALU.add).then_inc(mm_free, 1)

            def step(b, experts=True, ahead=True):
                for p in range(4):
                    clip(b, p)
                if experts:
                    x1_lo(b, b - 1, 0)
                    x1_lo(b, b - 1, 1)
                if ahead:
                    hs_lo(b, b + 1, 0)
                    hs_lo(b, b + 1, 1)
                clip(b, 4)
                clip(b, 5)
                if experts:
                    router(b, b - 1, 0)
                clip(b, 6)
                clip(b, 7)
                if ahead:
                    hs_lo(b, b + 1, 2)
                    hs_lo(b, b + 1, 3)
                if experts:
                    x1_lo(b, b - 1, 2)
                    x1_lo(b, b - 1, 3)
                normalise(b, ["00", "01"])
                normalise(b, ["10", "11"])
                if experts:
                    gating(b, b - 1, 0)
                if ahead:
                    query_lo(b, b + 1, 0)
                att_lo(b, 0)
                att_lo(b, 1)
                normalise(b, ["20", "21"])
                if experts:
                    router(b, b - 1, 1)
                    hid_lo(b, b - 1, 0)
                normalise(b, ["30", "31"])
                if experts:
                    gating(b, b - 1, 1)
                centre(b, (0, 1))
                att_lo(b, 2)
                att_lo(b, 3)
                if ahead:
                    query_lo(b, b + 1, 1)
                if experts:
                    hid_lo(b, b - 1, 1)
                    for t in range(NT):
                        finish(b, b - 1, t)
                residual(b, (0, 1))
                centre(b, (2, 3))
                if ahead:
                    query_lo(b, b + 1, 2)
                residual(b, (2, 3))
                if ahead:
                    query_lo(b, b + 1, 3)

            dve.memset(exp_min[:, :], EXP_LO).then_inc(rs_step, 1)
            dve.memset(eps_sb[:, :], EPS).then_inc(rs_step, 1)
            dve.wait_ge(x0_in, 16 * NT)
            ln_stats(range(NT))
            dve.wait_ge(wq_in, 16)
            for c in range(KC):
                dve.wait_ge(wq_hi_ok, c + 1)
                dve.tensor_tensor(wq_lo[:, c, :], wq_raw[:, c, :], wq_hi[:, c, :].bitcast(F32), ALU.subtract
                                  ).then_inc(wq_lo_ok, 1)
            for t in range(NT):
                hs_lo(BEFORE, 0, t)
            dve.wait_ge(ctx_in, 16)
            dve.tensor_scalar(ctx_lim[:, :, :], ctx_sb[:, :, :], -LIM, LIM, ALU.max, ALU.min).then_inc(ctx_part, 1)
            dve.tensor_tensor(ctx_notnan[:, :, :], ctx_sb[:, :, :], ctx_sb[:, :, :], ALU.is_equal
                              ).then_inc(ctx_part, 1)
            dve.wait_ge(small_in, SMALL)
            query_lo(BEFORE, 0, 0)
            dve.tensor_scalar(ctx_finite[:, :, :], ctx_sb[:, :, :], 0.0, 0.0, ALU.mult, ALU.is_equal
                              ).then_inc(ctx_part, 1)
            dve.wait_ge(zeroed, 3)
            dve.wait_ge(ctx_part, 3)
            dve.copy_predicated(ctx_clean[:, :, :], ctx_notnan[:, :, :], ctx_lim[:, :, :]).then_inc(ctx_part, 1)
            query_lo(BEFORE, 0, 1)
            dve.wait_ge(ctx_part, 4)
            dve.copy_predicated(ctx_clean[:, :, :], ctx_finite[:, :, :], ctx_sb[:, :, :]).then_inc(ctx_ok, 1)
            query_lo(BEFORE, 0, 2)
            dve.tensor_scalar(rs_sb[:, :], rs_raw[:, :], 0.0, RES_SCALE_MAX, ALU.max, ALU.min).then_inc(rs_step, 1)
            dve.wait_ge(rs_step, 3)
            dve.tensor_scalar(rs_sq[:, :], rs_sb[:, :], rs_sb[:, :], None, ALU.mult).then_inc(rs_step, 1)
            dve.tensor_scalar(gamma_rs[:, :], gamma_bc[:, :], rs_sb[:, :], None, ALU.mult).then_inc(rs_step, 1)
            query_lo(BEFORE, 0, 3)
            dve.wait_ge(mask_in, 32)
            dve.tensor_scalar(attend[:, :], mask_sb[:, :], 0.5, None, ALU.is_gt).then_inc(mask_step, 1)
            dve.wait_ge(mask_step, 1)
            dve.tensor_scalar(exp_max[:, :], attend[:, :], EXP_HI - EXP_LO, EXP_LO, ALU.mult, ALU.add
                              ).then_inc(mask_step, 1)
            dve.wait_ge(zeroed, 5)
            dve.tensor_copy(bo_hl[0:1, :], bo_raw[0:1, :]).then_inc(bo_step, 1)
            dve.tensor_copy(bo_hi32[32:33, :], bo_raw[32:33, :]).then_inc(bo_step, 1)
            dve.tensor_copy(ones_k[:, :], ones_f[:, :]).then_inc(ones_ok, 1)
            dve.wait_ge(xr_in, 16)
            ln_stats(range(NT, B * NT))
            for m in range(KC):
                key_lo(m)
            dve.wait_ge(bo_step, 2)
            dve.tensor_tensor(bo_hl[32:33, :], bo_raw[32:33, :], bo_hi32[32:33, :].bitcast(F32), ALU.subtract
                              ).then_inc(bo_step, 1)
            dve.wait_ge(vones_ok, 2)
            for j in range(2):
                value_blocks(j)
            dve.wait_ge(mask_step, 2)
            dve.wait_ge(rs_step, 5)
            step(0, experts=False)
            with dve.Fori(1, B - 1, 1) as b:
                step(b)
            step(B - 1, ahead=False)
            x1_lo(AFTER, B - 1, 0)
            x1_lo(AFTER, B - 1, 1)
            router(AFTER, B - 1, 0)
            gating(AFTER, B - 1, 0)
            x1_lo(AFTER, B - 1, 2)
            x1_lo(AFTER, B - 1, 3)
            router(AFTER, B - 1, 1)
            gating(AFTER, B - 1, 1)
            hid_lo(AFTER, B - 1, 0)
            finish(AFTER, B - 1, 0)
            finish(AFTER, B - 1, 1)
            hid_lo(AFTER, B - 1, 1)
            finish(AFTER, B - 1, 2)
            finish(AFTER, B - 1, 3)

        @block.gpsimd
        def _(pool):
            def ln_power(i, some):
                pool.wait_ge(ln_ve_ok, 2 * i + 2)
                pool.tensor_tensor(ln_rstd[:, some], ln_ve[:, some], minus_half[:, some], ALU.pow
                                   ).then_inc(ln_rstd_ok, 1)
                pool.wait_ge(ln_rstd_ok, 2 * i + 1)
                pool.tensor_tensor(ln_bias[:, some], ln_nm[:, some], ln_rstd[:, some], ALU.mult
                                   ).then_inc(ln_rstd_ok, 1)

            def key_blocks(bb, *before):
                cols = bass.ts(bb, T)
                for semaphore, value in before:
                    pool.wait_ge(semaphore, value)
                for h in range(4):
                    r = slice(HD * h, HD * (h + 1))
                    pool.tensor_copy(kbd[r, :, h // 2, T * (h % 2):T * (h % 2) + T],
                                     k_hl[r, :, :, cols].rearrange("p a c n -> p (a c) n")).then_inc(kbd_ok, 1)
                pool.wait_ge(kbd_ok, 4 * (bb + 1))

            def add_beta(bb):
                for t in range(NT):
                    xt = xs[:, NT * bb + t, :]
                    pool.tensor_tensor(xt, xt, beta_bc[:, :], ALU.add).then_inc(xb_ok, 1)

            def value_copy(b):
                pool.tensor_copy(vbd[:, :, :], vbd_all[:, b, :, :]).then_inc(vbd_ok, 1)

            def residual_powers(b, tiles):
                for t in tiles:
                    n = NT * b + t + 1
                    pool.wait_ge(d_ve_ok, n)
                    pool.tensor_tensor(d_rstd[:, t:t + 1], d_ve[:, t:t + 1], minus_half[:, 0:1], ALU.pow
                                       ).then_inc(d_rstd_ok, 1)
                for t in tiles:
                    n = NT * b + t + 1
                    pool.wait_ge(n_ve_ok, 2 * n)
                    pool.tensor_tensor(n_rstd[:, t:t + 1], n_ve[:, t:t + 1], minus_half[:, 0:1], ALU.pow
                                       ).then_inc(n_rstd_ok, 1)
                    pool.wait_ge(n_rstd_ok, 2 * n - 1)
                    pool.tensor_tensor(n_bias[:, t:t + 1], n_nm[:, t:t + 1], n_rstd[:, t:t + 1], ALU.mult
                                       ).then_inc(n_rstd_ok, 1)

            def rivals(bb, j):
                n, ts = 2 * bb + j + 1, slice(2 * j, 2 * j + 2)
                mine = lg[:, ts, :].unsqueeze(3).broadcast_to([P, 2, E, E])
                other = lg[:, ts, :].unsqueeze(2).broadcast_to([P, 2, E, E])
                pool.wait_ge(lg_ok, n)
                pool.tensor_tensor(diff[:, ts, :, :], other, mine, ALU.subtract).then_inc(diff_ok, 1)

            def step(b, experts=True, ahead=True):
                if experts:
                    rivals(b - 1, 0)
                if ahead:
                    pool.wait_ge(s_full, NP * b + NP)
                    key_blocks(b + 1, (diff_ok, 2 * b - 1) if experts else (vbd_ok, 1))
                    pool.wait_ge(hs_ok, NT * (b + 2))
                    add_beta(b + 1)
                if experts:
                    rivals(b - 1, 1)
                residual_powers(b, (0, 1))
                if ahead:
                    pool.wait_ge(v_full, ring_v.count(b, "v31"))
                    value_copy(b + 1)
                residual_powers(b, (2, 3))

            pool.memset(minus_half[:, :], -0.5).then_inc(half_ok, 1)
            pool.memset(ident[:, :], 0.0).then_inc(zeroed, 1)
            pool.memset(least[:, :, :], -FLT_MIN).then_inc(zeroed, 1)
            pool.memset(ctx_clean[:, :, :], 0.0).then_inc(zeroed, 1)
            pool.wait_ge(zeroed, 3)
            pool.affine_select(out=ident[:, :], in_=ident[:, :], compare_op=ALU.not_equal, fill=1.0, base=0,
                               pattern=[[-1, P]], channel_multiplier=1).then_inc(ident_ok, 1)
            pool.wait_ge(half_ok, 1)
            ln_power(0, slice(0, NT))
            pool.affine_select(out=least[:, :, :], in_=least[:, :, :], compare_op=ALU.is_gt, fill=0.0, base=0,
                               pattern=[[1, E], [-1, E]], channel_multiplier=0).then_inc(least_ok, 1)
            pool.memset(ones_f[:, :], 1.0).then_inc(zeroed, 1)
            pool.memset(bo_hl[:, :].bitcast(F32), 0.0).then_inc(zeroed, 1)
            pool.memset(kbd[:, :, :, :].bitcast(F32), 0.0).then_inc(zeroed, 1)
            pool.memset(vbd_all[:, :, :, :], 0.0).then_inc(zeroed, 1)
            pool.wait_ge(zeroed, 7)
            for s in range(2):
                pool.memset(vbd_all[s * T:(s + 1) * T, :, :, 2 * HD + s], ONE).then_inc(vones_ok, 1)
            pool.wait_ge(vones_ok, 2)
            pool.wait_ge(small_in, SMALL)
            pool.wait_ge(hs_ok, NT)
            add_beta(0)
            pool.wait_ge(wo_in, 16)
            for c in range(KC):
                pool.wait_ge(wo_hi_ok, c + 1)
                pool.tensor_tensor(wo_lo[:, c, :], wo_raw[:, c, :], wo_hi[:, c, :].bitcast(F32), ALU.subtract
                                   ).then_inc(wo_lo_ok, 1)
            pool.wait_ge(ffn_in, 48)
            pool.wait_ge(ffn_hi_ok, 2)
            pool.tensor_tensor(dr_lo[:, :, :], dr_raw[:, :, :], dr_hi[:, :, :].bitcast(F32), ALU.subtract
                               ).then_inc(ffn_lo_ok, 1)
            pool.tensor_tensor(up_lo[:, :], up_raw[:, :], up_hi[:, :].bitcast(F32), ALU.subtract
                               ).then_inc(ffn_lo_ok, 1)
            pool.wait_ge(ffn_lo_ok, 2)
            pool.wait_ge(mm_free, ring_r.count(BEFORE, "K3"))
            ln_power(1, slice(NT, B * NT))
            key_blocks(0, (ln_rstd_ok, 4), (ffn_lo_ok, 2))
            pool.wait_ge(mm_free, ring_r.count(BEFORE, "V1"))
            value_copy(0)
            pool.wait_ge(least_ok, 1)
            step(0, experts=False)
            with pool.Fori(1, B - 1, 1) as b:
                step(b)
            step(B - 1, ahead=False)
            rivals(B - 1, 0)
            rivals(B - 1, 1)


def _transposed(a):
    return np.ascontiguousarray(np.swapaxes(a, -1, -2))


def kernel(x, ctx_2048, mask_BxS2_ik0, L0_xattn_Wq, L0_xattn_bq, L0_xattn_Wk, L0_xattn_bk, L0_xattn_Wv, L0_xattn_bv,
           L0_xattn_Wo, L0_xattn_bo, L0_xattn_ln_gamma, L0_xattn_ln_beta, L0_xattn_residual_scale, L0_ffn_router_w,
           L0_ffn_down_w, L0_ffn_up_w):
    import concourse.bacc as bacc
    from concourse.bass_utils import run_bass_kernel_spmd

    a = lambda v: np.ascontiguousarray(np.asarray(v))
    H = x.shape[-1]
    arrays = {
        "x": a(x),
        "ctx_t": _transposed(a(ctx_2048).reshape(-1, H)),
        "mask_t": _transposed(a(mask_BxS2_ik0)),
        "wq_t": _transposed(a(L0_xattn_Wq)),
        "bq": _transposed(a(L0_xattn_bq).reshape(-1, P)),
        "wk_t": _transposed(a(L0_xattn_Wk)),
        "bk": _transposed(a(L0_xattn_bk).reshape(-1, P)),
        "wv_t": _transposed(a(L0_xattn_Wv)),
        "bv": a(L0_xattn_bv),
        "wo_t": _transposed(a(L0_xattn_Wo)),
        "bo": a(L0_xattn_bo),
        "gamma": a(L0_xattn_ln_gamma),
        "beta": a(L0_xattn_ln_beta),
        "rs": a(L0_xattn_residual_scale).reshape(1, 1),
        "router_t": _transposed(a(L0_ffn_router_w)),
        "down_t": _transposed(a(L0_ffn_down_w).reshape(-1, H)),
        "up_t": a(_transposed(a(L0_ffn_up_w))).reshape(-1, H),
    }
    nc = bacc.Bacc("TRN2", target_bir_lowering=False, num_devices=1)
    args = [nc.dram_tensor(n, v.shape, mybir.dt.from_np(v.dtype), kind="ExternalInput").ap() for n, v in arrays.items()]
    args.append(nc.dram_tensor("out", x.shape, mybir.dt.float32, kind="ExternalOutput").ap())
    build(nc, *args)
    r = run_bass_kernel_spmd(nc, [arrays], core_ids=[0])
    return r.results[0]["out"]
```

```python
from contextlib import ExitStack

import numpy as np

import concourse.bass as bass
from concourse import mybir

ALU = mybir.AluOpType
ACT = mybir.ActivationFunctionType
AX = mybir.AxisListType
F32 = mybir.dt.float32
F32R = mybir.dt.float32r
I32 = mybir.dt.int32
U8 = mybir.dt.uint8

P = 128
NH = 16
E = 8
EPS = 1e-5
RES_SCALE_MAX = 0.3
CLIP = 50.0
LIM = 10000.0
FLT_MAX = float(np.finfo(np.float32).max)
FLT_MIN = float(np.finfo(np.float32).tiny)

R_STEP = ["S0", "S1", "S2", "S3", "q2", "q3", "S4", "S5", "S6", "S7", "Q0", "W0", "W1", "Q1", "U0", "U1", "U2", "U3",
          "W2", "W3"]
T_STEP = ["n0", "n1", "h0", "h1", "h2", "h3", "n2", "n3", "c0", "c1", "a0", "c2", "c3", "a1"]
V_STEP = ["f0", "f1", "v00", "v01", "v10", "v11", "v20", "v21", "f2", "f3", "v30", "v31"]
R_LAST = ["S0", "S1", "S2", "S3", "q2", "q3", "S4", "S5", "S6", "S7", "W0", "W1", "U0", "U1", "W2", "W3", "U2", "U3"]
R_BEFORE = ["Q0", "Q1", "K0", "K1", "K2", "K3", "V0", "V1"]
T_BEFORE = ["h0", "h1", "h2", "h3"]
NEXT, PREVIOUS = "Qh", "nfaU"
CHUNK = ["Q0", "Q1", "q2", "q3"]
BEFORE, AFTER = -1, 4


class Ring:

    def __init__(self, banks, order, before=(), apart="", last=()):
        self.banks = banks
        self.apart = apart
        steps = range(AFTER)
        self.parts = {BEFORE: list(before)}
        for b in steps:
            self.parts[b] = [u for u in order if not (b == steps[0] and u[0] in PREVIOUS)
                             and not (b == steps[-1] and u[0] in NEXT)]
        self.parts[steps[-1]] = list(last) or self.parts[steps[-1]]
        self.parts[AFTER] = [u for u in order if u[0] in PREVIOUS]
        self.all = [(part, u) for part, uses in self.parts.items() for u in uses]

    def bank(self, part, use):
        if isinstance(part, int):
            return self.all.index((part, use)) % self.banks
        first, second = self.bank(1, use), self.bank(2, use)
        assert first == second
        return first

    def count(self, part, use):
        if isinstance(part, int):
            apart = use[0] == self.apart
            return sum((u[0] == self.apart) == apart for _, u in self.all[:self.all.index((part, use)) + 1])
        first, second = self.count(1, use), self.count(2, use)
        return (part - 1) * (second - first) + first

    def count_before(self, part, use):
        if isinstance(part, int):
            return self.count(part - 1, use)
        first, second = self.count(0, use), self.count(1, use)
        return (part - 1) * (second - first) + first

    def freed(self, part, use):
        if isinstance(part, int):
            at = self.all.index((part, use)) - self.banks
            return None if at < 0 else (self.all[at][1][0] == self.apart, self.count(*self.all[at]))
        (kind, first), (same_kind, second) = self.freed(1, use), self.freed(2, use)
        assert kind == same_kind
        return kind, (part - 1) * (second - first) + first


def build(nc, x, ctx_t, mask_t, wq_t, bq, wk_t, bk, wv_t, bv, wo_t, bo, gamma, beta, rs, router_t, down_t, up_t, out):
    B, S, H = x.shape
    T = ctx_t.shape[1] // B
    HD = H // NH
    EI = up_t.shape[0]
    EXP_I = EI // E
    KC = H // P
    NT = S // P
    NP = NH // 2
    VW = 2 * HD + 2
    FW = EI + E
    SCALE = 1.0 / float(np.sqrt(HD))
    EXP_HI = float(np.exp(np.float64(CLIP)))
    EXP_LO = float(np.exp(np.float64(-CLIP)))
    ONE = 1.0 + 1e-8
    assert T * 2 == P and H % P == 0 and S == NT * P and HD == 32 and NT == 4 and EI == P

    ring_r = Ring(4, R_STEP, R_BEFORE, apart="S", last=R_LAST)
    ring_t = Ring(2, T_STEP, T_BEFORE)
    ring_v = Ring(2, V_STEP)
    assert B == AFTER

    stack = ExitStack()
    with stack:
        def sb(name, shape, dt=F32):
            return stack.enter_context(nc.sbuf_tensor(name, shape, dt))

        def sem(name):
            return stack.enter_context(nc.semaphore(name))

        def split(name, shape):
            return sb(name + "_hi", shape, F32R), sb(name + "_lo", shape, F32R)

        xs = sb("xs", [P, B * NT, H])
        stage = sb("stage", [P, 2 * KC, H])
        wq_raw, wo_raw, probs = stage[:, 0:KC, :], stage[:, KC:, :], stage[:, :, :]
        wk = sb("wk", [P, KC, H])
        att, x1n = wk, wk
        wv = sb("wv", [P, KC, H])
        hs, cen = wv, wv
        ctx_sb = wo_raw[:, 0:2, :].rearrange("p a n -> p (a n)").rearrange("p (k n) -> p k n", k=KC)
        wq_hi, wq_lo = split("wq", [P, KC, H])
        wo_hi, wo_lo = split("wo", [P, KC, H])
        dr_raw = sb("dr_raw", [P, KC, FW])
        dr_flat = dr_raw[:, :, :].rearrange("p k n -> p (k n)")
        vbd = dr_flat[:, 0:NP * VW].rearrange("p (n w) -> p n w", n=NP)
        ctx_words = KC * B * T // 4
        ctx_notnan, ctx_finite = (
            dr_flat[:, i * ctx_words:(i + 1) * ctx_words].bitcast(U8).rearrange("p (k n) -> p k n", k=KC)
            for i in range(2))
        dr_hl = sb("dr_hl", [P, KC, 2, FW], F32R)
        dr_hi, dr_lo = dr_hl[:, :, 0, :], dr_hl[:, :, 1, :]
        up_raw = sb("up_raw", [EI, H])
        up_hi, up_lo = split("up", [EI, H])
        compare = sb("compare", [P, 4, NT * E * E])
        ctx_clean = compare[:, :, :]
        k_hl = sb("k_hl", [P, 2, KC, B * T], F32R)
        kbd = sb("kbd", [P, 2 * KC, 2, 2 * T], F32R)
        vbd_all = sb("vbd_all", [P, B, NP, VW])
        q_hi, q_lo = split("q", [P, KC, S])
        hst_hi, hst_lo = split("hst", [P, NT, KC, P])
        attt_hi, attt_lo = split("attt", [P, NT, KC, P])
        x1t_hi, x1t_lo = attt_hi, attt_lo
        hidden = sb("hidden", [P, NT * (EI + FW + EI)])
        hid_tanh = hidden[:, 0:NT * EI].rearrange("p (t n) -> p t n", t=NT)
        hid_lg = hidden[:, NT * EI:NT * (EI + FW)].rearrange("p (t n) -> p t n", t=NT)
        hid, lg = hid_lg[:, :, 0:EI], hid_lg[:, :, EI:FW]
        hid_out = hidden[:, NT * (EI + FW):]
        hidg = hid_out.rearrange("p (t n) -> p t n", t=NT)
        ctx_lim = hidden[:, 0:KC * B * T].rearrange("p (k n) -> p k n", k=KC)
        hidt_hi, hidt_lo = split("hidt", [EI, NT, P])

        ident = sb("ident", [P, P])
        least = sb("least", [P, E, E])
        ones_k = sb("ones_k", [33, P], F32R)
        ones_f = sb("ones_f", [33, P])
        bo_raw = hid_out[0:33, :]
        bo_hl = sb("bo_hl", [33, H], F32R)
        bo_hi32 = hidt_hi[0:33, :, :].rearrange("p t n -> p (t n)")
        gamma_bc = sb("gamma_bc", [P, H])
        gamma_rs = gamma_bc
        beta_bc = sb("beta_bc", [P, H])
        bv_bc = sb("bv_bc", [P, H])
        bq_sb = sb("bq_sb", [P, KC])
        bk_sb = sb("bk_sb", [P, KC])
        rs_raw = sb("rs_raw", [P, 1])
        act_first = sb("act_first", [P, 1])
        rs_sb = sb("rs_sb", [P, 1])
        rs_sq = sb("rs_sq", [P, 1])
        mask_sb = sb("mask_sb", [P, B], I32)
        attend = sb("attend", [P, B])
        exp_max = sb("exp_max", [P, B])
        exp_min = sb("exp_min", [P, 1])
        eps_sb = sb("eps_sb", [P, 1])
        minus_half = sb("minus_half", [P, B * NT])

        ln_st = sb("ln_st", [P, B * NT, 6])
        ln_mv = sb("ln_mv", [P, B * NT, 2])
        ln_ve = sb("ln_ve", [P, B * NT])
        ln_nm = sb("ln_nm", [P, B * NT])
        ln_rstd = sb("ln_rstd", [P, B * NT])
        ln_bias = sb("ln_bias", [P, B * NT])
        d_st = sb("d_st", [P, NT, 6])
        d_mv = sb("d_mv", [P, NT, 2])
        d_ve = sb("d_ve", [P, NT])
        d_rstd = sb("d_rstd", [P, NT])
        n_st = sb("n_st", [P, NT, 6])
        n_mv = sb("n_mv", [P, NT, 2])
        n_ve = sb("n_ve", [P, NT])
        n_rstd = sb("n_rstd", [P, NT])
        n_nm = sb("n_nm", [P, NT])
        n_bias = sb("n_bias", [P, NT])
        rz = sb("rz", [P, NT, 2, 4, 2])
        lmax = sb("lmax", [P, NT])
        lsub = sb("lsub", [P, NT, E])
        lexp = sb("lexp", [P, NT, E])
        diff, beats = (compare[:, i, :].rearrange("p (t e f) -> p t e f", t=NT, e=E) for i in range(2))
        rank = sb("rank", [P, NT, E])
        kept = sb("kept", [P, NT, E])
        lsum = sb("lsum", [P, NT])
        lrec = sb("lrec", [P, NT])
        gate = sb("gate", [P, NT, E])

        def banks(name, n):
            return [stack.enter_context(nc.psum_tensor(f"{name}{i}", [P, 512], F32)) for i in range(n)]

        ps_r, ps_t, ps_v = banks("ps_r", 4), banks("ps_t", 2), banks("ps_v", 2)

        x0_in, x0b_in, x1_in, xr_in, ctx_in, wq_in, wk_in, wv_in, wo_in, ffn_in, small_in, mask_in = [
            sem(n) for n in ("x0_in", "x0b_in", "x1_in", "xr_in", "ctx_in", "wq_in", "wk_in", "wv_in", "wo_in",
                             "ffn_in", "small_in", "mask_in")]
        stored = sem("stored")
        mm_full, mm_free, t_full, t_free = sem("mm_full"), sem("mm_free"), sem("t_full"), sem("t_free")
        s_full, v_full, v_free = sem("s_full"), sem("v_full"), sem("v_free")
        zeroed, ident_ok, half_ok, least_ok, ones_ok = (
            sem("zeroed"), sem("ident_ok"), sem("half_ok"), sem("least_ok"), sem("ones_ok"))
        bo_step, rs_step, mask_step, vones_ok = (
            sem("bo_step"), sem("rs_step"), sem("mask_step"), sem("vones_ok"))
        ctx_part, ctx_ok = sem("ctx_part"), sem("ctx_ok")
        wq_hi_ok, wq_lo_ok, wo_hi_ok, wo_lo_ok, ffn_hi_ok, ffn_lo_ok = [
            sem(n) for n in ("wq_hi_ok", "wq_lo_ok", "wo_hi_ok", "wo_lo_ok", "ffn_hi_ok", "ffn_lo_ok")]
        k_hi_ok, v_ok, kbd_ok, vbd_ok = sem("k_hi_ok"), sem("v_ok"), sem("kbd_ok"), sem("vbd_ok")
        ln_st_ok, ln_mv_ok, ln_ve_ok, ln_rstd_ok, hs_ok = (
            sem("ln_st_ok"), sem("ln_mv_ok"), sem("ln_ve_ok"), sem("ln_rstd_ok"), sem("hs_ok"))
        hst_hi_ok, q_hi_ok = sem("hst_hi_ok"), sem("q_hi_ok")
        exp_ok, probs_ok = sem("exp_ok"), sem("probs_ok")
        rz_ok = sem("rz_ok")
        attt_hi_ok = sem("attt_hi_ok")
        xb_ok = sem("xb_ok")
        d_st_ok, d_mv_ok, d_ve_ok, d_rstd_ok, x1_ok = (
            sem("d_st_ok"), sem("d_mv_ok"), sem("d_ve_ok"), sem("d_rstd_ok"), sem("x1_ok"))
        n_st_ok, n_mv_ok, n_ve_ok, n_rstd_ok, x1n_ok, x1t_hi_ok = (
            sem("n_st_ok"), sem("n_mv_ok"), sem("n_ve_ok"), sem("n_rstd_ok"), sem("x1n_ok"), sem("x1t_hi_ok"))
        tanh_ok, cross_ok, lmax_ok, lsub_ok, lexp_ok = (
            sem("tanh_ok"), sem("cross_ok"), sem("lmax_ok"), sem("lsub_ok"), sem("lexp_ok"))
        diff_ok, beats_ok, rank_ok, kept_ok, lsum_ok, lrec_ok, gate_ok, hid_ok, hidg_ok, hidt_hi_ok = [
            sem(n) for n in ("diff_ok", "beats_ok", "rank_ok", "kept_ok", "lsum_ok", "lrec_ok", "gate_ok",
                             "hid_ok", "hidg_ok", "hidt_hi_ok")]

        block = stack.enter_context(nc.Block())

        def wide(w):
            return w.rearrange("(k p) n -> p k n", p=P)

        x_tiles = x.rearrange("b (t p) h -> p (b t) h", p=P)
        out_tiles = out.rearrange("b (t p) h -> p (b t) h", p=P)
        SMALL = 16 * 8

        @block.sync
        def _(sp):
            sp.dma_start(xs[:, 0:2, :], x_tiles[:, 0:2, :]).then_inc(x0_in, 16)
            sp.dma_start(xs[:, 2:NT, :], x_tiles[:, 2:NT, :]).then_inc(x0b_in, 16)
            sp.dma_start(wq_raw[:, :, :], wide(wq_t)).then_inc(wq_in, 16)
            sp.dma_start(ctx_sb[:, :, :], wide(ctx_t)).then_inc(ctx_in, 16)
            sp.dma_start(wk[:, :, :], wide(wk_t)).then_inc(wk_in, 16)
            sp.dma_start(xs[:, NT:2 * NT, :], x_tiles[:, NT:2 * NT, :]).then_inc(x1_in, 16)
            sp.wait_ge(t_full, NT)
            sp.dma_start(wv[:, :, :], wide(wv_t)).then_inc(wv_in, 16)
            sp.wait_ge(ctx_ok, 1)
            sp.dma_start(wo_raw[:, :, :], wide(wo_t)).then_inc(wo_in, 16)
            sp.dma_start(dr_raw[:, :, 0:EI], wide(down_t)).then_inc(ffn_in, 16)
            sp.dma_start(dr_raw[:, :, EI:FW], wide(router_t)).then_inc(ffn_in, 16)
            sp.dma_start(up_raw[:, :], up_t).then_inc(ffn_in, 16)
            sp.dma_start(xs[:, 2 * NT:, :], x_tiles[:, 2 * NT:, :]).then_inc(xr_in, 16)

            def store(part, bb):
                for t in range(NT):
                    sp.wait_ge(mm_free, ring_r.count(part, f"U{t}"))
                    sp.dma_start(out_tiles[:, bass.ds(NT * bb + t, 1), :],
                                 xs[:, bass.ds(NT * bb + t, 1), :]).then_inc(stored, 16)

            with sp.Fori(1, B - 1, 1) as b:
                store(b, b - 1)
            store(B - 1, B - 2)
            store(AFTER, B - 1)
            sp.wait_ge(stored, 16 * B * NT)

        def rows(v, n):
            return v.rearrange("(a h) -> a h", a=1).broadcast_to([n, H])

        @block.tensor
        def _(pe):
            def passes(dst, pairs, start=True, stop=True):
                n = len(pairs)
                for i, (w, m) in enumerate(pairs):
                    last = pe.matmul(dst, w, m, start=start and i == 0, stop=stop and i == n - 1)
                return last

            def three(hi_w, lo_w, hi_m, lo_m):
                return [(hi_w, hi_m), (hi_w, lo_m), (lo_w, hi_m)]

            def take(ring, part, use, free=mm_free):
                freed = ring.freed(part, use)
                if freed:
                    pe.wait_ge(exp_ok if freed[0] else free, freed[1])
                return ring.bank(part, use)

            def transposes(part, use, src):
                bank = ps_t[take(ring_t, part, use, t_free)]
                for c in range(len(src)):
                    mmi = pe.transpose(bank[:, c * P:(c + 1) * P], src[c], ident[:, :])
                mmi.then_inc(t_full, 1)

            def chunks(buffer, t):
                return [buffer[:, t, c * P:(c + 1) * P] for c in range(KC)]

            def hs_transpose(part, bb, t):
                pe.wait_ge(hs_ok, NT * bb + t + 1)
                transposes(part, f"h{t}", chunks(hs, t))

            def query(part, m):
                k = take(ring_r, part, CHUNK[m])
                if m == 0:
                    pe.wait_ge(t_free, ring_t.count(part, "h3"))
                pairs = []
                for c in range(KC):
                    cols = slice(m * P, (m + 1) * P)
                    pairs += three(wq_hi[:, c, cols], wq_lo[:, c, cols], hst_hi[:, :, c, :], hst_lo[:, :, c, :])
                passes(ps_r[k][:, :], pairs).then_inc(mm_full, 1)

            def keys(m):
                k = take(ring_r, BEFORE, f"K{m}")
                passes(ps_r[k][:, 0:B * T], [(wk[:, c, m * P:(m + 1) * P], ctx_clean[:, c, :]) for c in range(KC)]
                       ).then_inc(mm_full, 1)

            def values(j):
                k = take(ring_r, BEFORE, f"V{j}")
                passes(ps_r[k][:, :], [(ctx_clean[:, c, j * P:(j + 1) * P], wv[:, c, :]) for c in range(KC)]
                       ).then_inc(mm_full, 1)

            def scores(b, p):
                k = take(ring_r, b, f"S{p}")
                c, i = p // 2, p % 2
                passes(ps_r[k][:, :],
                       three(kbd[:, c, i, :], kbd[:, KC + c, i, :], q_hi[:, c, :], q_lo[:, c, :])).then_inc(s_full, 1)

            def weigh(b, t, g):
                k = take(ring_v, b, f"v{t}{g}", v_free)
                if t == 0:
                    pe.wait_ge(probs_ok, NP * b + 4 * g + 4)
                for i in range(4):
                    p = 4 * g + i
                    mmi = pe.matmul(ps_v[k][:, i * VW:(i + 1) * VW], probs[:, p, t * P:(t + 1) * P],
                                    vbd[:, p, :], start=True, stop=True)
                mmi.then_inc(v_full, 1)

            def att_transpose(b, t):
                pe.wait_ge(v_free, ring_v.count(b, f"v{t}1"))
                transposes(b, f"c{t}", chunks(att, t))

            def project(b, t):
                pe.wait_ge(t_free, ring_t.count(b, f"c{t}"))
                k = take(ring_r, b, f"W{t}")
                pairs = [(ones_k[:, :], bo_hl[:, :])]
                for c in range(KC):
                    pairs += three(attt_hi[:, t, c, :], attt_lo[:, t, c, :], wo_hi[:, c, :], wo_lo[:, c, :])
                passes(ps_r[k][:, :], pairs).then_inc(mm_full, 1)

            def x1n_transpose(part, bb, t):
                pe.wait_ge(x1n_ok, NT * bb + t + 1)
                transposes(part, f"n{t}", chunks(x1n, t))

            def down(part, j):
                for t in (2 * j, 2 * j + 1):
                    k = take(ring_v, part, f"f{t}", v_free)
                    pe.wait_ge(t_free, ring_t.count(part, f"n{t}"))
                    both, cross = ps_v[k][:, 0:2 * FW], ps_v[k][:, FW:2 * FW]
                    for c in range(KC):
                        last = c == KC - 1
                        if last:
                            pe.matmul(cross, x1t_lo[:, t, c, :], dr_hi[:, c, :], start=False, stop=False)
                        mmi = pe.matmul(both, x1t_hi[:, t, c, :], dr_hl[:, c, :, :].rearrange("p a n -> p (a n)"),
                                        start=c == 0, stop=last)
                        if not last:
                            pe.matmul(cross, x1t_lo[:, t, c, :], dr_hi[:, c, :], start=False, stop=False)
                    mmi.then_inc(v_full, 1)

            def hid_transpose(part, bb, j):
                pe.wait_ge(hidg_ok, 2 * bb + j + 1)
                transposes(part, f"a{j}", [hidg[:, 2 * j + i, :] for i in range(2)])

            def up(part, t):
                if t % 2 == 0:
                    pe.wait_ge(t_free, ring_t.count(part, f"a{t // 2}"))
                k = take(ring_r, part, f"U{t}")
                passes(ps_r[k][:, :], three(hidt_hi[:, t, :], hidt_lo[:, t, :], up_hi[:, :], up_lo[:, :])
                       ).then_inc(mm_full, 1)

            def step(b, experts=True, ahead=True):
                pe.wait_ge(kbd_ok, 4 * (b + 1))
                scores(b, 0)
                scores(b, 1)
                if experts:
                    x1n_transpose(b, b - 1, 0)
                    x1n_transpose(b, b - 1, 1)
                scores(b, 2)
                scores(b, 3)
                query(b, 2)
                query(b, 3)
                pe.wait_ge(mm_free, ring_r.count(b, "q2"))
                scores(b, 4)
                scores(b, 5)
                if experts:
                    down(b, 0)
                pe.wait_ge(mm_free, ring_r.count(b, "q3"))
                scores(b, 6)
                scores(b, 7)
                if ahead:
                    hs_transpose(b, b + 1, 0)
                    hs_transpose(b, b + 1, 1)
                pe.wait_ge(vbd_ok, b + 1)
                weigh(b, 0, 0)
                weigh(b, 0, 1)
                if ahead:
                    hs_transpose(b, b + 1, 2)
                    hs_transpose(b, b + 1, 3)
                weigh(b, 1, 0)
                weigh(b, 1, 1)
                if experts:
                    x1n_transpose(b, b - 1, 2)
                    x1n_transpose(b, b - 1, 3)
                if ahead:
                    query(b, 0)
                att_transpose(b, 0)
                att_transpose(b, 1)
                weigh(b, 2, 0)
                weigh(b, 2, 1)
                project(b, 0)
                if experts:
                    down(b, 1)
                    hid_transpose(b, b - 1, 0)
                weigh(b, 3, 0)
                weigh(b, 3, 1)
                project(b, 1)
                att_transpose(b, 2)
                att_transpose(b, 3)
                if ahead:
                    query(b, 1)
                if ahead and experts:
                    hid_transpose(b, b - 1, 1)
                    for t in range(NT):
                        up(b, t)
                elif experts:
                    up(b, 0)
                    up(b, 1)
                    hid_transpose(b, b - 1, 1)
                project(b, 2)
                project(b, 3)
                if not ahead:
                    up(b, 2)
                    up(b, 3)

            pe.wait_ge(ident_ok, 1)
            for t in range(NT):
                hs_transpose(BEFORE, 0, t)
            pe.wait_ge(wq_hi_ok, KC)
            pe.wait_ge(wq_lo_ok, KC)
            for m in range(2):
                query(BEFORE, m)
            pe.wait_ge(ctx_ok, 1)
            pe.wait_ge(wk_in, 16)
            for m in range(KC):
                keys(m)
            pe.wait_ge(wv_in, 16)
            for j in range(2):
                values(j)
            pe.wait_ge(wo_hi_ok, KC)
            pe.wait_ge(wo_lo_ok, KC)
            pe.wait_ge(bo_step, 3)
            pe.wait_ge(ones_ok, 1)
            step(0, experts=False)
            pe.wait_ge(ffn_hi_ok, 2)
            pe.wait_ge(ffn_lo_ok, 2)
            with pe.Fori(1, B - 1, 1) as b:
                step(b)
            step(B - 1, ahead=False)
            x1n_transpose(AFTER, B - 1, 0)
            x1n_transpose(AFTER, B - 1, 1)
            down(AFTER, 0)
            x1n_transpose(AFTER, B - 1, 2)
            x1n_transpose(AFTER, B - 1, 3)
            down(AFTER, 1)
            hid_transpose(AFTER, B - 1, 0)
            up(AFTER, 0)
            up(AFTER, 1)
            hid_transpose(AFTER, B - 1, 1)
            up(AFTER, 2)
            up(AFTER, 3)

        @block.scalar
        def _(act):
            def hi(part, use, dst, done):
                act.wait_ge(t_full, ring_t.count(part, use))
                c = dst.shape[1]
                act.copy(dst, ps_t[ring_t.bank(part, use)][:, 0:c * P].rearrange("p (c n) -> p c n", c=c)
                         ).then_inc(done, 1)

            def hs_norm(bb, t):
                if isinstance(bb, int) and bb == 0:
                    act.wait_ge(ln_rstd_ok, 2 * (t // 2) + 2)
                else:
                    act.wait_ge(ln_rstd_ok, 6 if isinstance(bb, int) and bb == 1 else 10)
                if not (isinstance(bb, int) and bb < 2):
                    act.wait_ge(x1_ok, NT * (bb - 2) + t + 1)
                tile = NT * bb + t
                act.activation(hs[:, t, :], xs[:, bass.ds(tile, 1), :], ACT.Identity,
                               bias=ln_bias[:, bass.ds(tile, 1)], scale=ln_rstd[:, bass.ds(tile, 1)]
                               ).then_inc(hs_ok, 1)

            def x1_norm(bb, t):
                act.wait_ge(n_rstd_ok, 2 * (NT * bb + t + 1))
                act.activation(x1n[:, t, :], xs[:, NT * bb + t, :], ACT.Identity, bias=n_bias[:, t:t + 1],
                               scale=n_rstd[:, t:t + 1]).then_inc(x1n_ok, 1)

            def query_hi(part, m):
                act.wait_ge(mm_full, ring_r.count(part, CHUNK[m]))
                act.activation(q_hi[:, m, :], ps_r[ring_r.bank(part, CHUNK[m])][:, :], ACT.Identity,
                               bias=bq_sb[:, m:m + 1]).then_inc(q_hi_ok, 1)

            def key_hi(m):
                act.wait_ge(mm_full, ring_r.count(BEFORE, f"K{m}"))
                act.activation(k_hl[:, 0, m, :], ps_r[ring_r.bank(BEFORE, f"K{m}")][:, 0:B * T], ACT.Identity,
                               bias=bk_sb[:, m:m + 1]).then_inc(k_hi_ok, 1)

            def exp_scores(b, p):
                act.wait_ge(s_full, NP * b + p + 1)
                act.activation(probs[:, p, :], ps_r[ring_r.bank(b, f"S{p}")][:, :], ACT.Exp, scale=SCALE
                               ).then_inc(exp_ok, 1)

            def hs_hi(part, t):
                hi(part, f"h{t}", hst_hi[:, t, :, :], hst_hi_ok)

            def att_hi(b, t):
                hi(b, f"c{t}", attt_hi[:, t, :, :], attt_hi_ok)

            def x1_hi(part, t):
                hi(part, f"n{t}", x1t_hi[:, t, :, :], x1t_hi_ok)

            def hid_hi(part, j):
                hi(part, f"a{j}", hidt_hi[:, 2 * j:2 * j + 2, :], hidt_hi_ok)

            def hidden_tanh(part, j):
                act.wait_ge(v_free, ring_v.count(part, f"f{2 * j + 1}"))
                act.activation(hid_tanh[:, 2 * j:2 * j + 2, :], hid[:, 2 * j:2 * j + 2, :], ACT.Tanh, scale=0.5
                               ).then_inc(tanh_ok, 1)

            def exp_logits(bb, j):
                act.wait_ge(lsub_ok, 2 * bb + j + 1)
                act.activation(lexp[:, 2 * j:2 * j + 2, :], lsub[:, 2 * j:2 * j + 2, :], ACT.Exp).then_inc(lexp_ok, 1)

            def key_blocks(bb):
                cols = bass.ts(bb, T)
                for h in range(4):
                    r = slice(HD * h, HD * (h + 1))
                    act.copy(kbd[r, :, h // 2, T * (h % 2):T * (h % 2) + T],
                             k_hl[r, :, :, cols].rearrange("p a c n -> p (a c) n")).then_inc(kbd_ok, 1)

            def value_copy(bb):
                act.copy(vbd[:, :, :], vbd_all[:, bass.ds(bb, 1), :, :].rearrange("p b n w -> p (b n) w")
                         ).then_inc(vbd_ok, 1)

            def step(b, experts=True, ahead=True):
                exp_scores(b, 0)
                exp_scores(b, 1)
                if experts:
                    x1_hi(b, 0)
                    x1_hi(b, 1)
                exp_scores(b, 2)
                exp_scores(b, 3)
                query_hi(b, 2)
                query_hi(b, 3)
                if ahead:
                    hs_norm(b + 1, 0)
                    hs_norm(b + 1, 1)
                exp_scores(b, 4)
                exp_scores(b, 5)
                exp_scores(b, 6)
                exp_scores(b, 7)
                if ahead:
                    hs_hi(b, 0)
                    hs_hi(b, 1)
                if not experts:
                    act.wait_ge(mm_free, ring_r.count(BEFORE, "V1"))
                    act.wait_ge(ffn_lo_ok, 1)
                    value_copy(0)
                if ahead:
                    hs_norm(b + 1, 2)
                    hs_norm(b + 1, 3)
                    hs_hi(b, 2)
                    hs_hi(b, 3)
                if experts:
                    hidden_tanh(b, 0)
                    exp_logits(b - 1, 0)
                    x1_norm(b - 1, 2)
                    x1_norm(b - 1, 3)
                    x1_hi(b, 2)
                    x1_hi(b, 3)
                if ahead:
                    query_hi(b, 0)
                att_hi(b, 0)
                att_hi(b, 1)
                if ahead:
                    act.wait_ge(s_full, NP * b + NP)
                    key_blocks(b + 1)
                if experts:
                    hidden_tanh(b, 1)
                    exp_logits(b - 1, 1)
                    hid_hi(b, 0)
                att_hi(b, 2)
                att_hi(b, 3)
                if ahead:
                    act.wait_ge(v_full, ring_v.count(b, "v31"))
                    value_copy(b + 1)
                    query_hi(b, 1)
                if experts:
                    hid_hi(b, 1)
                x1_norm(b, 0)
                x1_norm(b, 1)

            act.wait_ge(rs_step, 1)
            act.activation(act_first[:, :], exp_min[:, :], ACT.Exp)
            hs_norm(0, 0)
            hs_norm(0, 1)
            hs_hi(BEFORE, 0)
            hs_norm(0, 2)
            hs_hi(BEFORE, 1)
            hs_norm(0, 3)
            hs_hi(BEFORE, 2)
            hs_hi(BEFORE, 3)
            act.dma_start(bq_sb[:, :], bq).then_inc(small_in, 16)
            act.dma_start(bk_sb[:, :], bk).then_inc(small_in, 16)
            act.dma_start(rs_raw[:, :], rs.broadcast_to([P, 1])).then_inc(small_in, 16)
            act.dma_start(bo_raw[0:1, :], rows(bo, 1)).then_inc(small_in, 16)
            act.dma_start(bo_raw[32:33, :], rows(bo, 1)).then_inc(small_in, 16)
            for half in range(2):
                act.dma_start(mask_sb[half * T:(half + 1) * T, :], mask_t).then_inc(mask_in, 16)
            act.dma_start(gamma_bc[:, :], rows(gamma, P)).then_inc(small_in, 16)
            act.dma_start(beta_bc[:, :], rows(beta, P)).then_inc(small_in, 16)
            act.dma_start(bv_bc[:, :], rows(bv, P)).then_inc(small_in, 16)
            act.wait_ge(small_in, SMALL)
            for m in range(2):
                query_hi(BEFORE, m)
            act.wait_ge(wo_in, 16)
            for c in range(KC):
                act.copy(wo_hi[:, c, :], wo_raw[:, c, :]).then_inc(wo_hi_ok, 1)
                key_hi(c)
            act.wait_ge(ffn_in, 48)
            act.copy(dr_hi[:, :, :], dr_raw[:, :, :]).then_inc(ffn_hi_ok, 1)
            act.wait_ge(zeroed, 7)
            act.wait_ge(mm_free, ring_r.count(BEFORE, "K3"))
            key_blocks(0)
            act.copy(up_hi[:, :], up_raw[:, :]).then_inc(ffn_hi_ok, 1)
            act.wait_ge(wq_lo_ok, KC)
            act.wait_ge(wo_lo_ok, KC)
            step(0, experts=False)
            with act.Fori(1, B - 1, 1) as b:
                step(b)
            step(B - 1, ahead=False)
            x1_hi(AFTER, 0)
            x1_hi(AFTER, 1)
            x1_norm(B - 1, 2)
            x1_norm(B - 1, 3)
            hidden_tanh(AFTER, 0)
            exp_logits(B - 1, 0)
            x1_hi(AFTER, 2)
            x1_hi(AFTER, 3)
            hid_hi(AFTER, 0)
            hidden_tanh(AFTER, 1)
            exp_logits(B - 1, 1)
            hid_hi(AFTER, 1)

        @block.vector
        def _(dve):
            def hold(semaphore, value):
                dve.wait_ge(semaphore, value)
                dve.nop(nofuse=True)

            def ln_stats(tiles):
                for t in tiles:
                    dve.bn_stats(ln_st[:, t, :], xs[:, t, :]).then_inc(ln_st_ok, 1)
                for t in tiles:
                    dve.wait_ge(ln_st_ok, t + 1)
                    dve.bn_aggr(ln_mv[:, t, :], ln_st[:, t, :]).then_inc(ln_mv_ok, 1)
                some = slice(tiles[0], tiles[-1] + 1)
                dve.wait_ge(ln_mv_ok, tiles[-1] + 1)
                dve.tensor_scalar(ln_ve[:, some], ln_mv[:, some, 1], EPS, None, ALU.add).then_inc(ln_ve_ok, 1)
                dve.tensor_scalar(ln_nm[:, some], ln_mv[:, some, 0], -1.0, None, ALU.mult).then_inc(ln_ve_ok, 1)

            def lo(part, use, dst, hi_part, hi_ok, n):
                dve.wait_ge(hi_ok, n)
                c = dst.shape[1]
                src = ps_t[ring_t.bank(part, use)][:, 0:c * P].rearrange("p (c n) -> p c n", c=c)
                dve.tensor_tensor(dst, src, hi_part.bitcast(F32), ALU.subtract).then_inc(t_free, 1)

            def hs_lo(part, bb, t):
                lo(part, f"h{t}", hst_lo[:, t, :, :], hst_hi[:, t, :, :], hst_hi_ok, NT * bb + t + 1)

            def att_lo(b, t):
                lo(b, f"c{t}", attt_lo[:, t, :, :], attt_hi[:, t, :, :], attt_hi_ok, NT * b + t + 1)

            def x1_lo(part, bb, t):
                lo(part, f"n{t}", x1t_lo[:, t, :, :], x1t_hi[:, t, :, :], x1t_hi_ok, NT * bb + t + 1)

            def hid_lo(part, bb, j):
                ts = slice(2 * j, 2 * j + 2)
                lo(part, f"a{j}", hidt_lo[:, ts, :], hidt_hi[:, ts, :], hidt_hi_ok, 2 * bb + j + 1)

            def query_lo(part, bb, m):
                dve.wait_ge(q_hi_ok, KC * bb + m + 1)
                dve.scalar_tensor_tensor(q_lo[:, m, :], ps_r[ring_r.bank(part, CHUNK[m])][:, :], bq_sb[:, m:m + 1],
                                         q_hi[:, m, :].bitcast(F32), ALU.add, ALU.subtract).then_inc(mm_free, 1)

            def key_lo(m):
                dve.wait_ge(k_hi_ok, m + 1)
                dve.scalar_tensor_tensor(k_hl[:, 1, m, :], ps_r[ring_r.bank(BEFORE, f"K{m}")][:, 0:B * T],
                                         bk_sb[:, m:m + 1], k_hl[:, 0, m, :].bitcast(F32), ALU.add, ALU.subtract
                                         ).then_inc(mm_free, 1)

            def value_blocks(j):
                bank = ps_r[ring_r.bank(BEFORE, f"V{j}")]
                dve.wait_ge(mm_full, ring_r.count(BEFORE, f"V{j}"))
                for i in range(2):
                    for s in range(2):
                        rows_in, rows_out = slice(i * T, (i + 1) * T), slice(s * T, (s + 1) * T)
                        src = bank[rows_in, :].rearrange("p (n s d) -> p n s d", s=2, d=HD)[:, :, s, :]
                        bias = bv_bc[rows_in, :].rearrange("p (n s d) -> p n s d", s=2, d=HD)[:, :, s, :]
                        final = (i, s) == (1, 1)
                        if final:
                            dve.wait_ge(v_ok, 3 * (j + 1))
                        dve.tensor_tensor(vbd_all[rows_out, 2 * j + i, :, s * HD:(s + 1) * HD], src, bias, ALU.add
                                          ).then_inc(mm_free if final else v_ok, 1)

            def clip(b, p):
                dve.wait_ge(exp_ok, NP * b + p + 1)
                dve.tensor_scalar(probs[:, p, :], probs[:, p, :], exp_min[:, 0:1], exp_max[:, bass.ds(b, 1)],
                                  ALU.max, ALU.min).then_inc(probs_ok, 1)

            def normalise(b, halves):
                def values_of(half):
                    return ps_v[ring_v.bank(b, f"v{half}")][:, 0:4 * VW].rearrange("p (n w) -> p n w", n=4)

                def reciprocals(half):
                    t, g = int(half[0]), int(half[1])
                    dve.wait_ge(v_full, ring_v.count(b, f"v{half}"))
                    dve.reciprocal(rz[:, t, g, :, :], values_of(half)[:, :, 2 * HD:VW]).then_inc(rz_ok, 1)

                def product(half):
                    t, g = int(half[0]), int(half[1])
                    order = [u[1:] for u in V_STEP if u[0] == "v"]
                    dve.wait_ge(rz_ok, 2 * NT * b + order.index(half) + 1)
                    dve.tensor_tensor(att[:, t, 4 * 2 * HD * g:4 * 2 * HD * (g + 1)].rearrange(
                                          "p (n s d) -> p n s d", n=4, s=2),
                                      values_of(half)[:, :, 0:2 * HD].rearrange("p n (s d) -> p n s d", s=2),
                                      rz[:, t, g, :, :].unsqueeze(3).broadcast_to([P, 4, 2, HD]), ALU.mult
                                      ).then_inc(v_free, 1)

                reciprocals(halves[0])
                for half, following in zip(halves, halves[1:]):
                    reciprocals(following)
                    product(half)
                product(halves[-1])

            def centre(b, tiles):
                bank = {t: ps_r[ring_r.bank(b, f"W{t}")] for t in tiles}
                n = {t: NT * b + t + 1 for t in tiles}
                for t in tiles:
                    hold(mm_full, ring_r.count(b, f"W{t}"))
                    dve.bn_stats(d_st[:, t, :], bank[t][:, :]).then_inc(d_st_ok, 1)
                for t in tiles:
                    hold(d_st_ok, n[t])
                    dve.bn_aggr(d_mv[:, t, :], d_st[:, t, :]).then_inc(d_mv_ok, 1)
                for t in tiles:
                    dve.wait_ge(d_mv_ok, n[t])
                    dve.tensor_scalar(d_ve[:, t:t + 1], d_mv[:, t, 1:2], rs_sq[:, :], eps_sb[:, :], ALU.mult, ALU.add
                                      ).then_inc(d_ve_ok, 1)
                for t in tiles:
                    dve.scalar_tensor_tensor(cen[:, t, :], bank[t][:, :], d_mv[:, t, 0:1], gamma_rs[:, :],
                                             ALU.subtract, ALU.mult).then_inc(mm_free, 1)

            def residual(bb, tiles, centred):
                n = {t: NT * bb + t + 1 for t in tiles}
                x_tile = {t: xs[:, NT * bb + t, :] for t in tiles}
                dve.wait_ge(xb_ok, NT * bb + NT)
                for t in tiles:
                    dve.wait_ge(mm_free, centred[t])
                    dve.wait_ge(d_rstd_ok, n[t])
                    dve.scalar_tensor_tensor(x_tile[t], cen[:, t, :], d_rstd[:, t:t + 1], x_tile[t], ALU.mult, ALU.add
                                             ).then_inc(x1_ok, 1)
                for t in tiles:
                    hold(x1_ok, n[t])
                    dve.bn_stats(n_st[:, t, :], x_tile[t]).then_inc(n_st_ok, 1)
                for t in tiles:
                    hold(n_st_ok, n[t])
                    dve.bn_aggr(n_mv[:, t, :], n_st[:, t, :]).then_inc(n_mv_ok, 1)
                for t in tiles:
                    dve.wait_ge(n_mv_ok, n[t])
                    dve.tensor_scalar(n_nm[:, t:t + 1], n_mv[:, t, 0:1], -1.0, None, ALU.mult).then_inc(n_ve_ok, 1)
                    dve.tensor_scalar(n_ve[:, t:t + 1], n_mv[:, t, 1:2], EPS, None, ALU.add).then_inc(n_ve_ok, 1)

            def router(part, bb, j):
                n, ts = 2 * bb + j + 1, slice(2 * j, 2 * j + 2)
                for t in (2 * j, 2 * j + 1):
                    bank = ps_v[ring_v.bank(part, f"f{t}")]
                    dve.wait_ge(v_full, ring_v.count(part, f"f{t}"))
                    dve.tensor_copy(hid_lg[:, t, :], bank[:, FW:2 * FW]).then_inc(cross_ok, 1)
                    dve.wait_ge(cross_ok, NT * bb + t + 1)
                    dve.tensor_tensor(hid_lg[:, t, :], bank[:, 0:FW], hid_lg[:, t, :], ALU.add).then_inc(v_free, 1)
                dve.wait_ge(v_free, ring_v.count(part, f"f{2 * j + 1}"))
                dve.tensor_reduce(lmax[:, ts], lg[:, ts, :], AX.X, ALU.max).then_inc(lmax_ok, 1)
                dve.wait_ge(lmax_ok, n)
                dve.tensor_tensor(lsub[:, ts, :], lg[:, ts, :], lmax[:, ts].unsqueeze(2).broadcast_to([P, 2, E]),
                                  ALU.subtract).then_inc(lsub_ok, 1)

            def gating(part, bb, j):
                n, ts = 2 * bb + j + 1, slice(2 * j, 2 * j + 2)
                dve.wait_ge(tanh_ok, n)
                dve.scalar_tensor_tensor(hid[:, ts, :], hid_tanh[:, ts, :], 1.0, hid[:, ts, :], ALU.add, ALU.mult
                                         ).then_inc(hid_ok, 1)
                dve.wait_ge(diff_ok, n)
                dve.tensor_tensor(beats[:, ts, :, :], diff[:, ts, :, :],
                                  least[:, :, :].unsqueeze(1).broadcast_to([P, 2, E, E]), ALU.is_gt
                                  ).then_inc(beats_ok, 1)
                dve.wait_ge(lexp_ok, n)
                dve.tensor_reduce(lsum[:, ts], lexp[:, ts, :], AX.X, ALU.add).then_inc(lsum_ok, 1)
                dve.wait_ge(beats_ok, n)
                dve.tensor_reduce(rank[:, ts, :], beats[:, ts, :, :], AX.X, ALU.add).then_inc(rank_ok, 1)
                dve.wait_ge(lsum_ok, n)
                dve.reciprocal(lrec[:, ts], lsum[:, ts]).then_inc(lrec_ok, 1)
                dve.wait_ge(rank_ok, n)
                dve.scalar_tensor_tensor(kept[:, ts, :], rank[:, ts, :], 1.5, lexp[:, ts, :], ALU.is_lt, ALU.mult
                                         ).then_inc(kept_ok, 1)
                dve.wait_ge(kept_ok, n)
                dve.wait_ge(lrec_ok, n)
                dve.scalar_tensor_tensor(gate[:, ts, :], kept[:, ts, :], 0.5,
                                         lrec[:, ts].unsqueeze(2).broadcast_to([P, 2, E]), ALU.mult, ALU.mult
                                         ).then_inc(gate_ok, 1)
                dve.wait_ge(gate_ok, n)
                dve.wait_ge(hid_ok, n)
                dve.tensor_tensor(hidg[:, ts, :].rearrange("p t (e i) -> p t e i", e=E),
                                  hid[:, ts, :].rearrange("p t (e i) -> p t e i", e=E),
                                  gate[:, ts, :].unsqueeze(3).broadcast_to([P, 2, E, EXP_I]), ALU.mult
                                  ).then_inc(hidg_ok, 1)

            def finish(part, bb, t):
                dve.wait_ge(mm_full, ring_r.count(part, f"U{t}"))
                xt = xs[:, NT * bb + t, :]
                dve.tensor_tensor(xt, ps_r[ring_r.bank(part, f"U{t}")][:, :], xt, ALU.add).then_inc(mm_free, 1)

            def last_residual(part):
                residual(part - 1, (2, 3), {t: ring_r.count_before(part, f"W{t}") for t in (2, 3)})

            def step(b, experts=True, ahead=True):
                for p in range(4):
                    clip(b, p)
                if experts:
                    last_residual(b)
                query_lo(b, b, 2)
                if experts:
                    x1_lo(b, b - 1, 0)
                    x1_lo(b, b - 1, 1)
                query_lo(b, b, 3)
                clip(b, 4)
                clip(b, 5)
                if experts:
                    router(b, b - 1, 0)
                clip(b, 6)
                clip(b, 7)
                if ahead:
                    hs_lo(b, b + 1, 0)
                    hs_lo(b, b + 1, 1)
                normalise(b, ["00", "01"])
                if ahead:
                    hs_lo(b, b + 1, 2)
                    hs_lo(b, b + 1, 3)
                normalise(b, ["10", "11"])
                if experts:
                    x1_lo(b, b - 1, 2)
                    x1_lo(b, b - 1, 3)
                if experts:
                    gating(b, b - 1, 0)
                if ahead:
                    query_lo(b, b + 1, 0)
                att_lo(b, 0)
                att_lo(b, 1)
                if not experts:
                    dve.wait_ge(xr_in, 16)
                    ln_stats(range(2 * NT, 3 * NT))
                normalise(b, ["20", "21"])
                if experts:
                    router(b, b - 1, 1)
                    hid_lo(b, b - 1, 0)
                else:
                    ln_stats(range(3 * NT, B * NT))
                centre(b, (0,))
                normalise(b, ["30", "31"])
                if experts:
                    gating(b, b - 1, 1)
                if ahead:
                    centre(b, (1,))
                att_lo(b, 2)
                att_lo(b, 3)
                if ahead:
                    query_lo(b, b + 1, 1)
                    if experts:
                        hid_lo(b, b - 1, 1)
                        for t in range(NT):
                            finish(b, b - 1, t)
                    residual(b, (0, 1), {t: ring_r.count(b, f"W{t}") for t in (0, 1)})
                    centre(b, (2,))
                    centre(b, (3,))
                else:
                    centre(b, (1,))
                    finish(b, b - 1, 0)
                    finish(b, b - 1, 1)
                    hid_lo(b, b - 1, 1)
                    residual(b, (0, 1), {t: ring_r.count(b, f"W{t}") for t in (0, 1)})
                    centre(b, (2,))
                    centre(b, (3,))

            dve.memset(exp_min[:, :], EXP_LO).then_inc(rs_step, 1)
            dve.memset(eps_sb[:, :], EPS).then_inc(rs_step, 1)
            dve.wait_ge(x0_in, 16)
            ln_stats(range(2))
            dve.wait_ge(x0b_in, 16)
            ln_stats(range(2, NT))

            def wq_low(c):
                dve.wait_ge(wq_hi_ok, c + 1)
                dve.tensor_tensor(wq_lo[:, c, :], wq_raw[:, c, :], wq_hi[:, c, :].bitcast(F32), ALU.subtract
                                  ).then_inc(wq_lo_ok, 1)

            dve.wait_ge(wq_in, 16)
            for c in range(KC):
                dve.tensor_copy(wq_hi[:, c, :], wq_raw[:, c, :]).then_inc(wq_hi_ok, 1)
            wq_low(0)
            wq_low(1)
            hs_lo(BEFORE, 0, 0)
            wq_low(2)
            hs_lo(BEFORE, 0, 1)
            wq_low(3)
            hs_lo(BEFORE, 0, 2)
            hs_lo(BEFORE, 0, 3)
            dve.wait_ge(ctx_in, 16)
            dve.tensor_scalar(ctx_lim[:, :, :], ctx_sb[:, :, :], -LIM, LIM, ALU.max, ALU.min).then_inc(ctx_part, 1)
            dve.tensor_tensor(ctx_notnan[:, :, :], ctx_sb[:, :, :], ctx_sb[:, :, :], ALU.is_equal
                              ).then_inc(ctx_part, 1)
            dve.tensor_scalar(ctx_finite[:, :, :], ctx_sb[:, :, :], 0.0, 0.0, ALU.mult, ALU.is_equal
                              ).then_inc(ctx_part, 1)
            dve.wait_ge(zeroed, 3)
            dve.wait_ge(ctx_part, 3)
            dve.copy_predicated(ctx_clean[:, :, :], ctx_notnan[:, :, :], ctx_lim[:, :, :]).then_inc(ctx_part, 1)
            dve.wait_ge(ctx_part, 4)
            dve.copy_predicated(ctx_clean[:, :, :], ctx_finite[:, :, :], ctx_sb[:, :, :]).then_inc(ctx_ok, 1)
            dve.wait_ge(small_in, SMALL)
            query_lo(BEFORE, 0, 0)
            dve.tensor_scalar(rs_sb[:, :], rs_raw[:, :], 0.0, RES_SCALE_MAX, ALU.max, ALU.min).then_inc(rs_step, 1)
            dve.wait_ge(rs_step, 3)
            dve.tensor_scalar(rs_sq[:, :], rs_sb[:, :], rs_sb[:, :], None, ALU.mult).then_inc(rs_step, 1)
            dve.tensor_scalar(gamma_rs[:, :], gamma_bc[:, :], rs_sb[:, :], None, ALU.mult).then_inc(rs_step, 1)
            query_lo(BEFORE, 0, 1)
            dve.wait_ge(mask_in, 32)
            dve.tensor_scalar(attend[:, :], mask_sb[:, :], 0.5, None, ALU.is_gt).then_inc(mask_step, 1)
            dve.wait_ge(mask_step, 1)
            dve.tensor_scalar(exp_max[:, :], attend[:, :], EXP_HI - EXP_LO, EXP_LO, ALU.mult, ALU.add
                              ).then_inc(mask_step, 1)
            dve.wait_ge(zeroed, 5)
            dve.tensor_copy(bo_hl[0:1, :], bo_raw[0:1, :]).then_inc(bo_step, 1)
            dve.tensor_copy(bo_hi32[32:33, :], bo_raw[32:33, :]).then_inc(bo_step, 1)
            dve.tensor_copy(ones_k[:, :], ones_f[:, :]).then_inc(ones_ok, 1)
            dve.wait_ge(bo_step, 2)
            dve.tensor_tensor(bo_hl[32:33, :], bo_raw[32:33, :], bo_hi32[32:33, :].bitcast(F32), ALU.subtract
                              ).then_inc(bo_step, 1)
            for c in range(KC):
                dve.wait_ge(wo_hi_ok, c + 1)
                dve.tensor_tensor(wo_lo[:, c, :], wo_raw[:, c, :], wo_hi[:, c, :].bitcast(F32), ALU.subtract
                                  ).then_inc(wo_lo_ok, 1)
                key_lo(c)
            dve.wait_ge(x1_in, 16)
            ln_stats(range(NT, 2 * NT))
            dve.wait_ge(vones_ok, 2)
            for j in range(2):
                value_blocks(j)
            dve.wait_ge(mask_step, 2)
            dve.wait_ge(rs_step, 5)
            step(0, experts=False)
            with dve.Fori(1, B - 1, 1) as b:
                step(b)
            step(B - 1, ahead=False)
            x1_lo(AFTER, B - 1, 0)
            x1_lo(AFTER, B - 1, 1)
            last_residual(AFTER)
            finish(B - 1, B - 2, 2)
            finish(B - 1, B - 2, 3)
            router(AFTER, B - 1, 0)
            gating(AFTER, B - 1, 0)
            x1_lo(AFTER, B - 1, 2)
            x1_lo(AFTER, B - 1, 3)
            router(AFTER, B - 1, 1)
            hid_lo(AFTER, B - 1, 0)
            gating(AFTER, B - 1, 1)
            finish(AFTER, B - 1, 0)
            finish(AFTER, B - 1, 1)
            hid_lo(AFTER, B - 1, 1)
            finish(AFTER, B - 1, 2)
            finish(AFTER, B - 1, 3)

        @block.gpsimd
        def _(pool):
            def ln_power(i, some):
                pool.wait_ge(ln_ve_ok, 2 * i + 2)
                pool.tensor_tensor(ln_rstd[:, some], ln_ve[:, some], minus_half[:, some], ALU.pow
                                   ).then_inc(ln_rstd_ok, 1)
                pool.wait_ge(ln_rstd_ok, 2 * i + 1)
                pool.tensor_tensor(ln_bias[:, some], ln_nm[:, some], ln_rstd[:, some], ALU.mult
                                   ).then_inc(ln_rstd_ok, 1)

            def add_beta(bb):
                for t in range(NT):
                    xt = xs[:, NT * bb + t, :]
                    pool.tensor_tensor(xt, xt, beta_bc[:, :], ALU.add).then_inc(xb_ok, 1)

            def residual_powers(bb, tiles):
                for t in tiles:
                    pool.wait_ge(d_ve_ok, NT * bb + t + 1)
                    pool.tensor_tensor(d_rstd[:, t:t + 1], d_ve[:, t:t + 1], minus_half[:, 0:1], ALU.pow
                                       ).then_inc(d_rstd_ok, 1)

            def x1_powers(bb, tiles):
                for t in tiles:
                    n = NT * bb + t + 1
                    pool.wait_ge(n_ve_ok, 2 * n)
                    pool.tensor_tensor(n_rstd[:, t:t + 1], n_ve[:, t:t + 1], minus_half[:, 0:1], ALU.pow
                                       ).then_inc(n_rstd_ok, 1)
                    pool.wait_ge(n_rstd_ok, 2 * n - 1)
                    pool.tensor_tensor(n_bias[:, t:t + 1], n_nm[:, t:t + 1], n_rstd[:, t:t + 1], ALU.mult
                                       ).then_inc(n_rstd_ok, 1)

            def rivals(part, bb, j):
                ts = slice(2 * j, 2 * j + 2)
                mine = lg[:, ts, :].unsqueeze(3).broadcast_to([P, 2, E, E])
                other = lg[:, ts, :].unsqueeze(2).broadcast_to([P, 2, E, E])
                pool.wait_ge(v_free, ring_v.count(part, f"f{2 * j + 1}"))
                pool.tensor_tensor(diff[:, ts, :, :], other, mine, ALU.subtract).then_inc(diff_ok, 1)

            def step(b, experts=True, ahead=True):
                if experts:
                    x1_powers(b - 1, (2, 3))
                    rivals(b, b - 1, 0)
                if ahead:
                    pool.wait_ge(hs_ok, NT * (b + 2))
                    add_beta(b + 1)
                if experts:
                    rivals(b, b - 1, 1)
                if not experts:
                    ln_power(3, slice(2 * NT, 3 * NT))
                    ln_power(4, slice(3 * NT, B * NT))
                residual_powers(b, (0, 1))
                x1_powers(b, (0, 1))
                residual_powers(b, (2, 3))

            pool.memset(minus_half[:, :], -0.5).then_inc(half_ok, 1)
            pool.memset(ident[:, :], 0.0).then_inc(zeroed, 1)
            pool.memset(least[:, :, :], -FLT_MIN).then_inc(zeroed, 1)
            pool.memset(ctx_clean[:, :, :], 0.0).then_inc(zeroed, 1)
            pool.wait_ge(zeroed, 3)
            pool.affine_select(out=ident[:, :], in_=ident[:, :], compare_op=ALU.not_equal, fill=1.0, base=0,
                               pattern=[[-1, P]], channel_multiplier=1).then_inc(ident_ok, 1)
            pool.wait_ge(half_ok, 1)
            ln_power(0, slice(0, 2))
            ln_power(1, slice(2, NT))
            pool.affine_select(out=least[:, :, :], in_=least[:, :, :], compare_op=ALU.is_gt, fill=0.0, base=0,
                               pattern=[[1, E], [-1, E]], channel_multiplier=0).then_inc(least_ok, 1)
            pool.memset(ones_f[:, :], 1.0).then_inc(zeroed, 1)
            pool.memset(bo_hl[:, :].bitcast(F32), 0.0).then_inc(zeroed, 1)
            pool.memset(kbd[:, :, :, :].bitcast(F32), 0.0).then_inc(zeroed, 1)
            pool.memset(vbd_all[:, :, :, :], 0.0).then_inc(zeroed, 1)
            pool.wait_ge(zeroed, 7)
            for s in range(2):
                pool.memset(vbd_all[s * T:(s + 1) * T, :, :, 2 * HD + s], ONE).then_inc(vones_ok, 1)
            pool.wait_ge(vones_ok, 2)
            pool.wait_ge(small_in, SMALL)
            pool.wait_ge(hs_ok, NT)
            add_beta(0)
            ln_power(2, slice(NT, 2 * NT))
            pool.wait_ge(ffn_in, 48)
            pool.wait_ge(ffn_hi_ok, 1)
            pool.tensor_tensor(dr_lo[:, :, :], dr_raw[:, :, :], dr_hi[:, :, :].bitcast(F32), ALU.subtract
                               ).then_inc(ffn_lo_ok, 1)
            pool.wait_ge(ffn_hi_ok, 2)
            pool.tensor_tensor(up_lo[:, :], up_raw[:, :], up_hi[:, :].bitcast(F32), ALU.subtract
                               ).then_inc(ffn_lo_ok, 1)
            pool.wait_ge(least_ok, 1)
            step(0, experts=False)
            with pool.Fori(1, B - 1, 1) as b:
                step(b)
            step(B - 1, ahead=False)
            x1_powers(B - 1, (2, 3))
            rivals(AFTER, B - 1, 0)
            rivals(AFTER, B - 1, 1)


def _transposed(a):
    return np.ascontiguousarray(np.swapaxes(a, -1, -2))


def kernel(x, ctx_2048, mask_BxS2_ik0, L0_xattn_Wq, L0_xattn_bq, L0_xattn_Wk, L0_xattn_bk, L0_xattn_Wv, L0_xattn_bv,
           L0_xattn_Wo, L0_xattn_bo, L0_xattn_ln_gamma, L0_xattn_ln_beta, L0_xattn_residual_scale, L0_ffn_router_w,
           L0_ffn_down_w, L0_ffn_up_w):
    import concourse.bacc as bacc
    from concourse.bass_utils import run_bass_kernel_spmd

    a = lambda v: np.ascontiguousarray(np.asarray(v))
    H = x.shape[-1]
    arrays = {
        "x": a(x),
        "ctx_t": _transposed(a(ctx_2048).reshape(-1, H)),
        "mask_t": _transposed(a(mask_BxS2_ik0)),
        "wq_t": _transposed(a(L0_xattn_Wq)),
        "bq": _transposed(a(L0_xattn_bq).reshape(-1, P)),
        "wk_t": _transposed(a(L0_xattn_Wk)),
        "bk": _transposed(a(L0_xattn_bk).reshape(-1, P)),
        "wv_t": _transposed(a(L0_xattn_Wv)),
        "bv": a(L0_xattn_bv),
        "wo_t": _transposed(a(L0_xattn_Wo)),
        "bo": a(L0_xattn_bo),
        "gamma": a(L0_xattn_ln_gamma),
        "beta": a(L0_xattn_ln_beta),
        "rs": a(L0_xattn_residual_scale).reshape(1, 1),
        "router_t": _transposed(a(L0_ffn_router_w)),
        "down_t": _transposed(a(L0_ffn_down_w).reshape(-1, H)),
        "up_t": a(_transposed(a(L0_ffn_up_w))).reshape(-1, H),
    }
    nc = bacc.Bacc("TRN2", target_bir_lowering=False, num_devices=1)
    args = [nc.dram_tensor(n, v.shape, mybir.dt.from_np(v.dtype), kind="ExternalInput").ap() for n, v in arrays.items()]
    args.append(nc.dram_tensor("out", x.shape, mybir.dt.float32, kind="ExternalOutput").ap())
    build(nc, *args)
    r = run_bass_kernel_spmd(nc, [arrays], core_ids=[0])
    return r.results[0]["out"]
```
